# Optimizing a Trainium2 kernel written in Bass

```python
import numpy as np
import jax
import jax.numpy as jnp

def _softmax(x, axis=-1):
    return jax.nn.softmax(x, axis=axis)

def _gelu(x):
    return jax.nn.gelu(x, approximate=True)

def _silu(x):
    return jax.nn.silu(x)

def _sigmoid(x):
    return jax.nn.sigmoid(x)

def _layernorm(x, axis=-1, eps=1e-05):
    m = jnp.mean(x, axis=axis, keepdims=True)
    v = jnp.var(x, axis=axis, keepdims=True)
    return (x - m) / jnp.sqrt(v + eps)

def _scatter_add(tgt, idx, src, axis=0):
    return tgt.at[idx].add(src)

def _segment_sum(src, seg, n):
    return jax.ops.segment_sum(src, seg, n)
kernel_name = 'mk_seq_postln_d1_jaxref_r8_b4b476'

def setup_inputs(seed: int=0):
    np.random.seed(seed)
    _w = jnp.asarray

    def _L0_attn_setup():
        import jax, jax.numpy as jnp
        import numpy as np
        D = 128
        H = 16
        KVH = 4
        HD = D // H
        LAT = 32
        WIN = 32
        B, S = (1, 256)
        BASE_G, BASE_L = (1000000.0, 10000.0)
        EPS = 1e-06

        def rmsnorm(x, w):
            return x * jax.lax.rsqrt(jnp.mean(x * x, axis=-1, keepdims=True) + EPS) * w

        def qk_norm(x):
            return x * jax.lax.rsqrt(jnp.mean(x * x, axis=-1, keepdims=True) + EPS)

        def rope(x, base):
            s, hd = (x.shape[-2], x.shape[-1])
            inv_freq = 1.0 / base ** (jnp.arange(0, hd, 2, dtype=jnp.float32) / hd)
            freqs = jnp.arange(s, dtype=jnp.float32)[:, None] * inv_freq[None, :]
            cos, sin = (jnp.cos(freqs), jnp.sin(freqs))
            xe, xo = (x[..., ::2], x[..., 1::2])
            out = jnp.stack([xe * cos - xo * sin, xe * sin + xo * cos], axis=-1)
            return out.reshape(x.shape)

        def split_heads(x, n_heads):
            b, s, _ = x.shape
            return x.reshape(b, s, n_heads, HD).transpose(0, 2, 1, 3)

        def repeat_kv(x):
            return jnp.repeat(x, H // KVH, axis=1)

        def sdpa(q, k, v, mask):
            scores = jnp.einsum('bhqd,bhkd->bhqk', q, k) / np.sqrt(HD).astype(np.float32)
            scores = jnp.where(mask, scores, jnp.float32(-1e+30))
            probs = jax.nn.softmax(scores, axis=-1)
            return jnp.einsum('bhqk,bhkd->bhqd', probs, v)

        def merge_heads(x):
            b, h, s, hd = x.shape
            return x.transpose(0, 2, 1, 3).reshape(b, s, h * hd)

        def global_latent_attn(x, wq, w_kv_down, w_k_up, w_v_up, wo):
            q = split_heads(x @ wq, H)
            latent = x @ w_kv_down
            k = split_heads(latent @ w_k_up, KVH)
            v = split_heads(latent @ w_v_up, KVH)
            q, k = (rope(q, BASE_G), rope(k, BASE_G))
            q, k = (qk_norm(q), qk_norm(k))
            k, v = (repeat_kv(k), repeat_kv(v))
            i = jnp.arange(x.shape[1])
            causal = i[:, None] >= i[None, :]
            return merge_heads(sdpa(q, k, v, causal)) @ wo

        def local_gqa_attn(x, wq, wk, wv, wo):
            q = split_heads(x @ wq, H)
            k = split_heads(x @ wk, KVH)
            v = split_heads(x @ wv, KVH)
            q, k = (rope(q, BASE_L), rope(k, BASE_L))
            q, k = (qk_norm(q), qk_norm(k))
            k, v = (repeat_kv(k), repeat_kv(v))
            i = jnp.arange(x.shape[1])
            diff = i[:, None] - i[None, :]
            mask = (diff >= 0) & (diff < WIN)
            return merge_heads(sdpa(q, k, v, mask)) @ wo
        key = jax.random.key(seed)
        ks = jax.random.split(key, 12)
        std = 0.02
        return {'hidden': jax.random.normal(ks[0], (B, S, D), dtype=jnp.float32), 'norm1_w': jnp.ones((D,), jnp.float32), 'norm2_w': jnp.ones((D,), jnp.float32), 'g_wq': jax.random.normal(ks[1], (D, H * HD), jnp.float32) * std, 'g_kv_down': jax.random.normal(ks[2], (D, LAT), jnp.float32) * std, 'g_k_up': jax.random.normal(ks[3], (LAT, KVH * HD), jnp.float32) * std, 'g_v_up': jax.random.normal(ks[4], (LAT, KVH * HD), jnp.float32) * std, 'g_wo': jax.random.normal(ks[5], (D, D), jnp.float32) * std, 'l_wq': jax.random.normal(ks[6], (D, H * HD), jnp.float32) * std, 'l_wk': jax.random.normal(ks[7], (D, KVH * HD), jnp.float32) * std, 'l_wv': jax.random.normal(ks[8], (D, KVH * HD), jnp.float32) * std, 'l_wo': jax.random.normal(ks[9], (D, D), jnp.float32) * std}
    _L0_attn_in = _L0_attn_setup()

    def _L0_ffn_setup():
        import jax, jax.numpy as jnp
        import numpy as np
        TOP_K = 2
        key = jax.random.key(seed)
        ks = jax.random.split(key, 5)
        B, S, H, I, E = (4, 256, 128, 512, 8)
        scale_hi = (2.0 / (H + I)) ** 0.5
        scale_he = (2.0 / (H + E)) ** 0.5
        return {'x': jax.random.normal(ks[0], (B, S, H), dtype=jnp.float32), 'router_w': jax.random.normal(ks[1], (E, H), dtype=jnp.float32) * scale_he, 'gate_w': jax.random.normal(ks[2], (E, I, H), dtype=jnp.float32) * scale_hi, 'up_w': jax.random.normal(ks[3], (E, I, H), dtype=jnp.float32) * scale_hi, 'down_w': jax.random.normal(ks[4], (E, H, I), dtype=jnp.float32) * scale_hi}
    _L0_ffn_in = _L0_ffn_setup()
    _d = {'L0_attn_hidden': _L0_attn_in['hidden'], 'L0_attn_norm1_w': _L0_attn_in['norm1_w'], 'L0_attn_norm2_w': _L0_attn_in['norm2_w'], 'L0_attn_g_wq': _L0_attn_in['g_wq'], 'L0_attn_g_kv_down': _L0_attn_in['g_kv_down'], 'L0_attn_g_k_up': _L0_attn_in['g_k_up'], 'L0_attn_g_v_up': _L0_attn_in['g_v_up'], 'L0_attn_g_wo': _L0_attn_in['g_wo'], 'L0_attn_l_wq': _L0_attn_in['l_wq'], 'L0_attn_l_wk': _L0_attn_in['l_wk'], 'L0_attn_l_wv': _L0_attn_in['l_wv'], 'L0_attn_l_wo': _L0_attn_in['l_wo'], 'L0_ffn_router_w': _L0_ffn_in['router_w'], 'L0_ffn_gate_w': _L0_ffn_in['gate_w'], 'L0_ffn_up_w': _L0_ffn_in['up_w'], 'L0_ffn_down_w': _L0_ffn_in['down_w']}
    _x0 = _d['L0_attn_hidden']
    _d['L0_attn_hidden'] = jax.random.normal(jax.random.fold_in(jax.random.key(seed), 1), (4, 512, 128), dtype=_x0.dtype)
    del _x0
    return _d

def reference(L0_attn_hidden, L0_attn_norm1_w, L0_attn_norm2_w, L0_attn_g_wq, L0_attn_g_kv_down, L0_attn_g_k_up, L0_attn_g_v_up, L0_attn_g_wo, L0_attn_l_wq, L0_attn_l_wk, L0_attn_l_wv, L0_attn_l_wo, L0_ffn_router_w, L0_ffn_gate_w, L0_ffn_up_w, L0_ffn_down_w):

    def _L0_attn_ref(hidden, norm1_w, norm2_w, g_wq, g_kv_down, g_k_up, g_v_up, g_wo, l_wq, l_wk, l_wv, l_wo):
        import jax, jax.numpy as jnp
        import numpy as np
        D = 128
        H = 16
        KVH = 4
        HD = D // H
        LAT = 32
        WIN = 32
        B, S = (1, 256)
        BASE_G, BASE_L = (1000000.0, 10000.0)
        EPS = 1e-06

        def rmsnorm(x, w):
            return x * jax.lax.rsqrt(jnp.mean(x * x, axis=-1, keepdims=True) + EPS) * w

        def qk_norm(x):
            return x * jax.lax.rsqrt(jnp.mean(x * x, axis=-1, keepdims=True) + EPS)

        def rope(x, base):
            s, hd = (x.shape[-2], x.shape[-1])
            inv_freq = 1.0 / base ** (jnp.arange(0, hd, 2, dtype=jnp.float32) / hd)
            freqs = jnp.arange(s, dtype=jnp.float32)[:, None] * inv_freq[None, :]
            cos, sin = (jnp.cos(freqs), jnp.sin(freqs))
            xe, xo = (x[..., ::2], x[..., 1::2])
            out = jnp.stack([xe * cos - xo * sin, xe * sin + xo * cos], axis=-1)
            return out.reshape(x.shape)

        def split_heads(x, n_heads):
            b, s, _ = x.shape
            return x.reshape(b, s, n_heads, HD).transpose(0, 2, 1, 3)

        def repeat_kv(x):
            return jnp.repeat(x, H // KVH, axis=1)

        def sdpa(q, k, v, mask):
            scores = jnp.einsum('bhqd,bhkd->bhqk', q, k) / np.sqrt(HD).astype(np.float32)
            scores = jnp.where(mask, scores, jnp.float32(-1e+30))
            probs = jax.nn.softmax(scores, axis=-1)
            return jnp.einsum('bhqk,bhkd->bhqd', probs, v)

        def merge_heads(x):
            b, h, s, hd = x.shape
            return x.transpose(0, 2, 1, 3).reshape(b, s, h * hd)

        def global_latent_attn(x, wq, w_kv_down, w_k_up, w_v_up, wo):
            q = split_heads(x @ wq, H)
            latent = x @ w_kv_down
            k = split_heads(latent @ w_k_up, KVH)
            v = split_heads(latent @ w_v_up, KVH)
            q, k = (rope(q, BASE_G), rope(k, BASE_G))
            q, k = (qk_norm(q), qk_norm(k))
            k, v = (repeat_kv(k), repeat_kv(v))
            i = jnp.arange(x.shape[1])
            causal = i[:, None] >= i[None, :]
            return merge_heads(sdpa(q, k, v, causal)) @ wo

        def local_gqa_attn(x, wq, wk, wv, wo):
            q = split_heads(x @ wq, H)
            k = split_heads(x @ wk, KVH)
            v = split_heads(x @ wv, KVH)
            q, k = (rope(q, BASE_L), rope(k, BASE_L))
            q, k = (qk_norm(q), qk_norm(k))
            k, v = (repeat_kv(k), repeat_kv(v))
            i = jnp.arange(x.shape[1])
            diff = i[:, None] - i[None, :]
            mask = (diff >= 0) & (diff < WIN)
            return merge_heads(sdpa(q, k, v, mask)) @ wo
        x = hidden
        x = x + global_latent_attn(rmsnorm(x, norm1_w), g_wq, g_kv_down, g_k_up, g_v_up, g_wo)
        x = x + local_gqa_attn(rmsnorm(x, norm2_w), l_wq, l_wk, l_wv, l_wo)
        return x

    def _L0_ffn_ref(x, router_w, gate_w, up_w, down_w):
        import jax, jax.numpy as jnp
        import numpy as np
        TOP_K = 2
        B, S, H = x.shape
        E = router_w.shape[0]
        xf = x.reshape(-1, H)
        logits = xf @ router_w.T
        probs = jax.nn.softmax(logits, axis=-1)
        topk_p, topk_i = jax.lax.top_k(probs, TOP_K)
        topk_p = topk_p / topk_p.sum(axis=-1, keepdims=True)

        def body(out, inputs):
            e, gw, uw, dw = inputs
            sel = topk_i == e
            mask = sel.any(axis=-1)
            w_tok = (topk_p * sel).sum(axis=-1)
            cnt = mask.sum().astype(xf.dtype)
            mean_w = jnp.where(cnt > 0, w_tok.sum() / jnp.maximum(cnt, 1.0), 0.0)
            h = jax.nn.silu(xf @ gw.T) * (xf @ uw.T)
            eo = h @ dw.T
            out = out + mask[:, None].astype(xf.dtype) * eo * mean_w
            return (out, None)
        out0 = jnp.zeros_like(xf)
        out, _ = jax.lax.scan(body, out0, (jnp.arange(E), gate_w, up_w, down_w))
        return out.reshape(B, S, H)
    x = L0_attn_hidden
    x = _layernorm(x + _L0_attn_ref(x, L0_attn_norm1_w, L0_attn_norm2_w, L0_attn_g_wq, L0_attn_g_kv_down, L0_attn_g_k_up, L0_attn_g_v_up, L0_attn_g_wo, L0_attn_l_wq, L0_attn_l_wk, L0_attn_l_wv, L0_attn_l_wo), axis=-1)
    x = _layernorm(x + _L0_ffn_ref(x, L0_ffn_router_w, L0_ffn_gate_w, L0_ffn_up_w, L0_ffn_down_w), axis=-1)
    return x

_drawn_inputs = setup_inputs


def setup_inputs(seed=0):
    import zlib

    import numpy as np

    out = dict(_drawn_inputs(seed))
    spreads = {'L0_attn_norm1_w': (1.0, 0.6), 'L0_attn_norm2_w': (1.0, 0.6)}
    factors = {'L0_attn_g_wq': 8.0,
     'L0_attn_g_kv_down': 8.0,
     'L0_attn_g_k_up': 8.0,
     'L0_attn_g_v_up': 8.0,
     'L0_attn_g_wo': 8.0,
     'L0_attn_l_wq': 4.94,
     'L0_attn_l_wk': 3.898,
     'L0_attn_l_wv': 3.694,
     'L0_attn_l_wo': 3.381}
    for name, (base, spread) in spreads.items():
        noise = np.random.default_rng([zlib.crc32(name.encode()), seed]).standard_normal(out[name].shape)
        drawn = base * np.exp(spread * noise) if base else spread * noise
        out[name] = jnp.asarray(drawn.astype(out[name].dtype))
    for name, factor in factors.items():
        out[name] = (out[name] * factor).astype(out[name].dtype)
    return out
```

```python
from contextlib import ExitStack

import concourse.bass as bass
import numpy as np
from concourse import mybir

ALU = mybir.AluOpType
ACT = mybir.ActivationFunctionType
AX = mybir.AxisListType
F32 = mybir.dt.float32
F16 = mybir.dt.float16
I32 = mybir.dt.int32
U32 = mybir.dt.uint32

P = 128
D = 128
H, KVH, HD = 16, 4, 8
REP = H // KVH
LAT = 32
WIN = 32
B, S = 4, 512
T = B * S
QT = S // P
HALVES = 2
PASSES = B // HALVES
NH = H + KVH
E, F = 8, 512
FC = F // P
QKV = NH * HD + KVH * HD
TERMS = 4
HW = TERMS * HD
SCALE = float(np.float32(1.0) / np.sqrt(np.float32(HD)))
BASES = (1000000.0, 10000.0)
RMS_EPS, LN_EPS = 1e-6, 1e-5
MASKED = -30000.0
PAD = 64
BLK = 64
MB = S // BLK

ROW = 132
CAP = T + P
PADROW = E * CAP
TILES = (2 * T + E * (P - 1)) // P
assert TILES == 39

GROUPS = (24, MB)


def rope_tables():
    out = np.empty((P, 2, 2, QT, HD // 2), np.float32)
    for l, base in enumerate(BASES):
        inv = (np.float32(1.0) / np.power(np.float32(base), np.arange(0, HD, 2, dtype=np.float32) / np.float32(HD))).astype(np.float32)
        ang = (np.arange(S, dtype=np.float32)[:, None] * inv[None, :]).astype(np.float32)
        for n, f in enumerate((np.cos, np.sin)):
            out[:, l, n] = f(ang).astype(np.float32).reshape(QT, P, HD // 2).transpose(1, 0, 2)
    return out


def window_bias():
    key = np.arange(P)[:, None] - BLK
    diff = np.arange(BLK)[None, :] - key
    block = np.where((diff >= 0) & (diff < WIN), 0.0, MASKED).astype(np.float16)
    return np.ascontiguousarray(np.broadcast_to(block[:, None, :], (P, REP, BLK)).reshape(P, REP * BLK))


def constants():
    upper = np.triu(np.ones((P, P)), 1)
    shift = np.zeros((P, 4 * E), np.float32)
    shift[:, 0:E] = np.arange(E) * CAP
    shift[:, E:2 * E] = np.arange(E, 0, -1)
    shift[:, 2 * E] = T + np.arange(P)
    return {
        "rope": rope_tables(),
        "eye": np.eye(P, dtype=np.float32),
        "ones": np.ones((P, P), np.float32),
        "half": np.concatenate([np.eye(P), upper, np.ones((P, P))], 1).astype(np.float16),
        "window": window_bias(),
        "expert": shift,
        "tile_no": np.broadcast_to(np.arange(TILES, dtype=np.float32)[:, None], (P, TILES, E)).reshape(P, TILES * E).copy(),
        "ids": np.arange(T, dtype=np.float32).reshape(T // P, P).T.copy(),
    }


class Event:

    def __init__(self, sem, per, skip=0, start=0):
        self.sem, self.per, self.skip, self.start = sem, per, skip, start

    def at(self, it, k):
        return it * self.per + (self.start + self.skip + k)


class Chain:

    def __init__(self, eng, sem, it=0, per=0, base=0):
        self.eng, self.sem, self.it, self.per, self.n, self.base = eng, sem, it, per, 0, base

    def do(self, ins):
        ins.then_inc(self.sem, 1)
        self.n += 1

    def sync(self):
        self.eng.wait_ge(self.sem, self.it * self.per + (self.base + self.n))

    def step(self, ins):
        self.do(ins)
        self.sync()


def tell(eng, ins, event, it, k):
    ins.then_inc(event.sem, 1)
    eng.wait_ge(event.sem, event.at(it, k))


class Lease:

    def __init__(self, last, per_pass_last):
        self.event, self.k = last, per_pass_last
        self.before_pass = True

    def wait_free(self, pe, it):
        k = self.k - (self.event.per if self.before_pass else 0)
        assert self.event.skip + k >= 0
        pe.wait_ge(self.event.sem, self.event.at(it, k))

    def lend(self, event, k):
        self.event, self.k, self.before_pass = event, k, False


def block_program(nc: bass.Bass, x_tok, x_feat, w_qkv1, w_kv_down_t, w_kv_up, w_qkv2, wo, norm_w,
                  router_t, gate_t, up_t, down_t, rope, eye, ones, half, window, expert, tile_no, ids, out):
    rows = nc.dram_tensor("routed_rows", [E * CAP + P, ROW], F32, kind="Internal").ap()
    acc = nc.dram_tensor("residual_rows", [T + P, D], F32, kind="Internal").ap()

    with ExitStack() as ctx:
        def sb(name, shape, dt=F32):
            return ctx.enter_context(nc.sbuf_tensor(name, shape, dt))

        def sem(name):
            return ctx.enter_context(nc.semaphore(name))

        def events(name, per1, per2, start=0):
            sems = [sem(f"{name}{u}") for u in range(HALVES)]
            return [[Event(sems[u], per1 + per2, l * per1, start) for u in range(HALVES)] for l in range(2)]

        rope_sb = sb("rope_sb", [P, 2, 2, QT, HD // 2])
        eye_sb = sb("eye_sb", [P, P])
        ones_sb = sb("ones_sb", [P, P])
        half_sb = sb("half_sb", [P, 3, P], F16)
        window_sb = sb("window_sb", [P, REP * BLK], F16)
        expert_sb = sb("expert_sb", [P, 4 * E])
        tile_no_sb = sb("tile_no_sb", [P, TILES, E])
        ids_sb = sb("ids_sb", [P, T // P])
        wq1 = sb("wq1", [P, D])
        down_sb = sb("down_sb", [LAT, D])
        up_kv_sb = sb("up_kv_sb", [LAT, 2 * KVH * HD])
        wraw2 = sb("wraw2", [P, QKV])
        wqkv = sb("wqkv", [P, 2, QKV])
        wo_sb = sb("wo_sb", [P, 2, D])
        norm_sb = sb("norm_sb", [P, 2])
        router_sb = sb("router_sb", [P, E])
        gate_sb = sb("gate_sb", [P, E * F])
        up_sb = sb("up_sb", [P, E * F])
        mlp_down_sb = sb("mlp_down_sb", [P, E * FC * D])
        pad_rows = sb("pad_rows", [P, ROW])
        eye16, before16, ones16 = (half_sb[:, n, :] for n in range(3))

        x_in = [sb(f"x_in{u}", [P, QT, D]) for u in range(HALVES)]
        xT = [sb(f"xT{u}", [P, S]) for u in range(HALVES)]
        x2 = [sb(f"x2_{u}", [P, QT, D]) for u in range(HALVES)]
        x1 = [sb(f"x1_{u}", [P, QT, ROW]) for u in range(HALVES)]
        xsq = [sb(f"xsq{u}", [P, QT, D]) for u in range(HALVES)]
        raw = [sb(f"raw{u}", [P, QT, QKV]) for u in range(HALVES)]
        sq = [sb(f"sq{u}", [P, QT, NH * HD]) for u in range(HALVES)]
        ms = [sb(f"ms{u}", [P, QT, NH + 1]) for u in range(HALVES)]
        inv = [sb(f"inv{u}", [P, QT, NH + 1]) for u in range(HALVES)]
        t_a = sb("t_a", [P, QT * (NH + 1)])
        t_b = sb("t_b", [P, QT * (NH + 1)])
        qn = sb("qn", [P, QT, NH, HD])
        by_cos = sb("by_cos", [P, QT, NH, HD])
        by_sin = sb("by_sin", [P, QT, NH, HD])
        rot = sb("rot", [P, QT, NH, HD])
        qk16 = [sb(f"qk16_{u}", [P, QT, NH, TERMS, HD], F16) for u in range(HALVES)]
        qT = [sb(f"qT{u}", [P, REP, S], F16) for u in range(HALVES)]
        kT = [sb(f"kT{u}", [P, KVH, PAD + S], F16) for u in range(HALVES)]
        v1 = [sb(f"v1_{u}", [P, QT, KVH, 2, HW]) for u in range(HALVES)]
        v2 = [sb(f"v2_{u}", [P, MB, KVH, HW]) for u in range(HALVES)]
        PN = 6
        probs = [sb(f"probs{n}", [P, 1024]) for n in range(PN)]
        o_sb = [sb(f"o_sb{n}", [P, S]) for n in range(2)]
        rden = sb("rden", [P, QT * H])
        on = sb("on", [P, QT, D])
        oT = sb("oT", [P, S])
        z = sb("z", [P, QT, D])
        zc = sb("zc", [P, QT, D])
        ln_s = sb("ln_s", [P, 4, QT])
        x1T = sb("x1T", [P, S])
        lg = sb("lg", [P, QT, E])
        r_t = [sb(f"r_t{n}", [P, QT, E]) for n in range(4)]
        sel = [sb(f"sel{n}", [P, QT, E]) for n in range(2)]
        sel16 = sb("sel16", [P, QT, E], F16)
        r_s = sb("r_s", [P, 8, QT])
        run = sb("run", [P, QT + 1, E])
        wacc = sb("wacc", [P, QT, E])
        slot = [sb(f"slot{u}", [P, 2, QT], U32) for u in range(HALVES)]

        ps_s = ctx.enter_context(nc.psum_tensor("ps_s", [P, 2, 1024], F32))
        ps_o = ctx.enter_context(nc.psum_tensor("ps_o", [P, 2, 512], F32))
        ps_w = ctx.enter_context(nc.psum_tensor("ps_w", [P, 2, 512], F32))

        loaded = {n: sem(f"loaded_{n}") for n in ("consts", "attn", "mlp")}
        weights_ready = sem("weights_ready")
        fold_ready = sem("fold_ready")
        pad_set = sem("pad_set")
        x_loaded = [Event(sem(f"x_loaded{u}"), 32) for u in range(HALVES)]
        qkv_ready = events("qkv_ready", 2, 2)
        raw_ready = events("raw_ready", 2, 2)
        sq_ready = events("sq_ready", 2, 2)
        arg_ready = events("arg_ready", 1, 1, start=1)
        ln_ready = events("ln_ready", 1, 1)
        guess_ready = events("guess_ready", 1, 1)
        inv_ready = events("inv_ready", 1, 1)
        v_ready = events("v_ready", 1, 1, start=1)
        split_ready = events("split_ready", 1, 1, start=1)
        turned = events("turned", 3, 3)
        qT_a = events("qT_a", 1, 1)
        qT_b = events("qT_b", 1, 1)
        kT_ready = events("kT_ready", 1, 1)
        scores = Event(sem("scores"), 2 * sum(GROUPS))
        exped = Event(sem("exped"), 2 * sum(GROUPS), start=1)
        masked = [Event(sem(f"masked{u}"), GROUPS[0]) for u in range(HALVES)]
        pv = Event(sem("pv"), 2 * sum(GROUPS), start=1)
        o_out = events("o_out", 2, 4, start=1)
        o_turned = events("o_turned", 2, 4)
        on_part = events("on_part", 2, 4)
        on_turned = events("on_turned", 1, 1)
        oT_ready = events("oT_ready", 1, 1)
        proj_ready = events("proj_ready", 1, 1)
        x2_ready = [Event(sem(f"x2_ready{u}"), 1) for u in range(HALVES)]
        x2_turned = [Event(sem(f"x2_turned{u}"), 1) for u in range(HALVES)]
        x2T_ready = [Event(sem(f"x2T_ready{u}"), 1) for u in range(HALVES)]
        z_ready = [Event(sem(f"z_ready{u}"), 1) for u in range(HALVES)]
        zc_ready = [Event(sem(f"zc_ready{u}"), 1) for u in range(HALVES)]
        zsq_ready = [Event(sem(f"zsq_ready{u}"), 1) for u in range(HALVES)]
        zarg_ready = [Event(sem(f"zarg_ready{u}"), 1) for u in range(HALVES)]
        zln_ready = [Event(sem(f"zln_ready{u}"), 1) for u in range(HALVES)]
        zguess_ready = [Event(sem(f"zguess_ready{u}"), 1) for u in range(HALVES)]
        x1_ready = [Event(sem(f"x1_ready{u}"), 1, start=1) for u in range(HALVES)]
        x1_turned = [Event(sem(f"x1_turned{u}"), 1) for u in range(HALVES)]
        x1T_ready = [Event(sem(f"x1T_ready{u}"), 1) for u in range(HALVES)]
        logits_ready = [Event(sem(f"logits_ready{u}"), 1) for u in range(HALVES)]
        logits_out = [Event(sem(f"logits_out{u}"), 1, start=1) for u in range(HALVES)]
        gap_ready = [Event(sem(f"gap_ready{u}"), 1) for u in range(HALVES)]
        ratio_ready = [Event(sem(f"ratio_ready{u}"), 1) for u in range(HALVES)]
        sel_ready = [Event(sem(f"sel_ready{u}"), 1) for u in range(HALVES)]
        ranks_ready = [Event(sem(f"ranks_ready{u}"), 1) for u in range(HALVES)]
        ranks_out = [Event(sem(f"ranks_out{u}"), 1, start=1) for u in range(HALVES)]
        slots_ready = [Event(sem(f"slots_ready{u}"), 1) for u in range(HALVES)]
        scattered = [Event(sem(f"scattered{u}"), 2 * QT * 16) for u in range(HALVES)]
        stored = [Event(sem(f"stored{u}"), 16) for u in range(HALVES)]
        x1_free = [Event(sem(f"x1_free{u}"), 2, start=2) for u in range(HALVES)]
        dve_own = sem("dve_own")
        act_own = sem("act_own")
        pool_own = sem("pool_own")
        pool_passed = sem("pool_passed")

        first = {(0, 0): 0, (0, 1): GROUPS[0], (1, 0): 2 * GROUPS[0], (1, 1): 2 * GROUPS[0] + GROUPS[1]}
        LAG = 3

        te_sb = sb("te_sb", [P, TILES + 1], I32)
        row_sb = sb("row_sb", [P, TILES + 1], I32)
        end_sb = sb("end_sb", [P, E], I32)
        mean_w = sb("mean_w", [P, E])
        c_f = [sb(f"c_f{n}", [P, E]) for n in range(4)]
        c_i = sb("c_i", [P, E], I32)
        c_t = [sb(f"c_t{n}", [P, TILES, E]) for n in range(3)]
        c_r = [sb(f"c_r{n}", [P, TILES + 1]) for n in range(2)]
        xs = [sb(f"xs{n}", [P, ROW]) for n in range(2)]
        xsT = [sb(f"xsT{n}", [P, P]) for n in range(2)]
        idu = [sb(f"idu{n}", [P, 1], U32) for n in range(2)]
        ys = [sb(f"ys{n}", [P, D]) for n in range(2)]
        sg = [probs[n][:, 0:F] for n in range(2)]
        hid = [probs[2 + n][:, 0:F] for n in range(2)]
        hT = [probs[4 + n][:, 0:F] for n in range(2)]
        counted = sem("counted")
        wsum_ready = sem("wsum_ready")
        tables = sem("tables")
        padded = sem("padded")
        xs_loaded = [sem(f"xs_loaded{n}") for n in range(2)]
        xs_turned = sem("xs_turned")
        xsT_ready = sem("xsT_ready")
        idu_ready = sem("idu_ready")
        gu_ready = sem("gu_ready")
        silu_ready = sem("silu_ready")
        hid_ready = sem("hid_ready")
        hid_turned = sem("hid_turned")
        hT_ready = sem("hT_ready")
        y_ready = sem("y_ready")
        ys_ready = sem("ys_ready")
        added = sem("added")
        dump_set = sem("dump_set")
        fin_loaded = [sem(f"fin_loaded{u}") for u in range(B)]
        fin_c = sem("fin_c")
        fin_sq = sem("fin_sq")
        fin_arg = sem("fin_arg")
        fin_guess = sem("fin_guess")
        fin_ready = sem("fin_ready")
        fin_stored = sem("fin_stored")
        fin_z = [(x_in[0], x2[0]), (x_in[1], x2[1]), (z, zc), (xsq[0], xsq[1])]

        def groups1(n):
            c, g = divmod(n, 6)
            kt, js = [(0, (0, 1)), (0, (2, 3)), (1, (0, 1)), (1, (2, 3)), (2, (0, 1, 2, 3)), (3, (0, 1, 2, 3))][g]
            width = S - P * kt
            return kt, c, js, width, (512 if len(js) == 2 else width)

        def prob_heads(g, count, step, width):
            return probs[g % PN][:, 0:count * step].rearrange("p (h n) -> p h n", n=step)[:, :, 0:width]

        block = ctx.enter_context(nc.Block())

        @block.sync
        def _(sp):
            for dst, src in ((wq1[:, :], w_qkv1), (down_sb[:, :], w_kv_down_t), (up_kv_sb[:, :], w_kv_up),
                             (norm_sb[:, :], norm_w), (rope_sb[:, :, :, :, :], rope), (eye_sb[:, :], eye),
                             (half_sb[:, :, :], half.rearrange("p (n m) -> p n m", n=3)), (wraw2[:, :], w_qkv2)):
                sp.dma_start(dst, src).then_inc(loaded["consts"], 16)
            for u in range(HALVES):
                sp.sem_inc(x1_free[u].sem, 1)
            with sp.Fori(0, PASSES) as it:
                for u in range(HALVES):
                    sp.wait_ge(x1_ready[u].sem, x1_ready[u].at(it, 0))
                    tok = (it * HALVES + u) * S
                    sp.dma_start(x_in[u][:, :, :], x_tok[bass.ds(tok, S), :].rearrange("(t p) d -> p t d", p=P)).then_inc(x_loaded[u].sem, 16)
                    sp.dma_start(xT[u][:, :], x_feat[:, bass.ds(tok, S)]).then_inc(x_loaded[u].sem, 16)
                for u in range(HALVES):
                    sp.wait_ge(x1_ready[u].sem, x1_ready[u].at(it, 1))
                    tok = (it * HALVES + u) * S
                    sp.dma_start(acc[bass.ds(tok, S), :].rearrange("(t p) d -> p t d", p=P), x1[u][:, :, 0:D]).then_inc(stored[u].sem, 16)
                for u in range(HALVES):
                    sp.wait_ge(stored[u].sem, stored[u].at(it, 16))
                    sp.sem_inc(x1_free[u].sem, 1)
            sp.wait_ge(pad_set, 1)
            sp.dma_start(rows[PADROW:PADROW + P, :], pad_rows[:, :]).then_inc(padded, 16)
            sp.dma_start(acc[T:T + P, :], pad_rows[:, 0:D]).then_inc(dump_set, 16)
            sp.wait_ge(tables, 1)
            for u in range(HALVES):
                sp.wait_ge(scattered[u].sem, scattered[u].per * PASSES)
            for e in range(E):
                end = sp.value_load(end_sb[0:1, e:e + 1], min_val=e * CAP, max_val=e * CAP + T)
                sp.dma_start(rows[bass.ds(end, P), :], pad_rows[:, :]).then_inc(padded, 16)
            sp.wait_ge(tables, 2)
            sp.wait_ge(padded, 16 * (E + 1))

            def load_tile(i, n):
                row = sp.value_load(row_sb[0:1, bass.ds(i, 1)], min_val=0, max_val=PADROW)
                sp.dma_start(xs[n][:, :], rows[bass.ds(row, P), :]).then_inc(xs_loaded[n], 16)

            load_tile(0, 0)
            load_tile(1, 1)
            with sp.Fori(0, (TILES - 1) // 2) as k:
                for n in range(2):
                    sp.wait_ge(xs_turned, 2 * k + (n + 1))
                    sp.wait_ge(idu_ready, 2 * k + (n + 1))
                    load_tile(2 * k + (n + 2), n)
            sp.wait_ge(added, 16 * TILES)
            for b in range(B):
                sp.dma_start(fin_z[b][0][:, :, :], acc[b * S:(b + 1) * S, :].rearrange("(t p) d -> p t d", p=P)).then_inc(fin_loaded[b], 16)
            for b in range(B):
                sp.wait_ge(fin_ready, b + 1)
                sp.dma_start(out[b, :, :].rearrange("(t p) d -> p t d", p=P), fin_z[b][0][:, :, :]).then_inc(fin_stored, 16)
            sp.wait_ge(fin_stored, 16 * B)
            for u in range(HALVES):
                sp.wait_ge(stored[u].sem, stored[u].per * PASSES)

        @block.gpsimd
        def _(pool):
            for u in range(HALVES):
                nc.gpsimd.memset(kT[u][:, :, :].bitcast(F32), 0.0).then_inc(pool_own, 1)
                nc.gpsimd.memset(v2[u][:, :, :, :], 0.0).then_inc(pool_own, 1)
                nc.gpsimd.memset(v1[u][:, :, :, :, :], 0.0).then_inc(pool_own, 1)
            pool.wait_ge(pool_own, 6)
            for u in range(HALVES):
                nc.gpsimd.memset(v1[u][:, :, :, 0, HD:HD + 1], 1.0).then_inc(pool_own, 1)
                nc.gpsimd.memset(v1[u][:, :, :, 1, 3 * HD:3 * HD + 1], 1.0).then_inc(pool_own, 1)
                nc.gpsimd.memset(v2[u][:, 1:MB, :, HD:HD + 1], 1.0).then_inc(pool_own, 1)
            pool.wait_ge(pool_own, 12)
            for u in range(HALVES):
                nc.gpsimd.memset(v2[u][BLK:P, 0:1, :, HD:HD + 1], 1.0).then_inc(pool_own, 1)
            pool.wait_ge(pool_own, 14)
            pool.dma_start(gate_sb[:, :], gate_t).then_inc(loaded["mlp"], 16)
            pool.dma_start(up_sb[:, :], up_t).then_inc(loaded["mlp"], 16)
            pool.dma_start(mlp_down_sb[:, :], down_t).then_inc(loaded["mlp"], 16)

            def masks(it, u):
                for n in range(GROUPS[0]):
                    kt, c, js, width, step = groups1(n)
                    g = first[0, u] + n
                    pool.wait_ge(exped.sem, exped.at(it, g + 1))
                    pool.sem_inc(pool_passed, 1)
                    tri = prob_heads(g, len(js), step, P)
                    nc.gpsimd.affine_select(out=tri, in_=tri, compare_op=ALU.is_ge, fill=0.0, base=0,
                                            pattern=[[0, len(js)], [1, P]], channel_multiplier=-1).then_inc(masked[u].sem, 1)

            def scatter(it, u):
                pool.wait_ge(slots_ready[u].sem, slots_ready[u].at(it, 1))
                pool.sem_inc(pool_passed, 1)
                for t in range(QT):
                    for k in range(2):
                        nc.gpsimd.indirect_dma_start(rows, bass.IndirectOffsetOnAxis(ap=slot[u][:, k, t:t + 1], axis=0),
                                                     x1[u][:, t, :], None).then_inc(scattered[u].sem, 16)

            for u in range(HALVES):
                pool.sem_inc(x1_free[u].sem, 1)
            with pool.Fori(0, PASSES) as it:
                masks(it, 0)
                masks(it, 1)
                scatter(it, 0)
                scatter(it, 1)
                for u in range(HALVES):
                    pool.wait_ge(scattered[u].sem, scattered[u].at(it, scattered[u].per))
                    pool.sem_inc(x1_free[u].sem, 1)

            for u in range(HALVES):
                pool.wait_ge(stored[u].sem, stored[u].per * PASSES)

            def add_tile(i, n, first=False):
                pool.wait_ge(ys_ready, i + 1)
                if not first:
                    pool.wait_ge(added, 16 * i)
                pool.sem_inc(pool_passed, 1)
                nc.gpsimd.indirect_dma_start(acc, bass.IndirectOffsetOnAxis(ap=idu[n][:, 0:1], axis=0), ys[n][:, :], None,
                                             compute_op=ALU.add).then_inc(added, 16)

            pool.wait_ge(dump_set, 16)
            add_tile(0, 0, first=True)
            with pool.Fori(0, (TILES - 1) // 2) as k:
                for n in (1, 2):
                    add_tile(2 * k + n, n % 2)

        @block.tensor
        def _(pe):
            pe.wait_ge(loaded["consts"], 16 * CONSTS)
            nc.tensor.matmul(ps_w[:, 0, 0:2 * KVH * HD], down_sb[:, :], up_kv_sb[:, :], start=True, stop=True).then_inc(fold_ready, 1)

            w = [Lease(ranks_out[1], 1), Lease(logits_out[1], 1)]
            o = [Lease(o_out[1][1], 4), Lease(o_out[1][1], 4)]

            def turn_x2(it, u):
                pe.wait_ge(x2_ready[u].sem, x2_ready[u].at(it, 1))
                w[0].wait_free(pe, it)
                for t in range(QT):
                    last = nc.tensor.transpose(ps_w[:, 0, P * t:P * t + P], x2[u][:, t, :], eye_sb[:, :])
                last.then_inc(x2_turned[u].sem, 1)
                w[0].lend(x2T_ready[u], 1)

            def project(it, l, u):
                if l == 0:
                    pe.wait_ge(x_loaded[u].sem, x_loaded[u].at(it, 32))
                else:
                    pe.wait_ge(x2T_ready[u].sem, x2T_ready[u].at(it, 1))
                for n in range(2):
                    w[n].wait_free(pe, it)
                    for t in range(2):
                        tile = 2 * n + t
                        last = nc.tensor.matmul(ps_w[:, n, 256 * t:256 * t + QKV], xT[u][:, P * tile:P * tile + P],
                                                wqkv[:, l, :], start=True, stop=True)
                    last.then_inc(qkv_ready[l][u].sem, 1)
                    w[n].lend(raw_ready[l][u], n + 1)

            def turn_heads(it, l, u):
                pe.wait_ge(split_ready[l][u].sem, split_ready[l][u].at(it, 1))
                flat = qk16[u][:, :, :, :, :].rearrange("p t h m d -> p t (h m d)")
                for n in range(2):
                    w[n].wait_free(pe, it)
                    bank = ps_w[:, n, :].bitcast(F16)
                    for t in range(2):
                        for c in range(REP):
                            last = nc.tensor.transpose(bank[:, 256 * c + P * t:256 * c + P * t + P],
                                                       flat[:, 2 * n + t, P * c:P * c + P], eye16)
                    last.then_inc(turned[l][u].sem, 1)
                    w[n].lend((qT_a, qT_b)[n][l][u], 1)
                w[0].wait_free(pe, it)
                bank = ps_w[:, 0, :].bitcast(F16)
                for t in range(QT):
                    last = nc.tensor.transpose(bank[:, P * t:P * t + P], flat[:, t, REP * P:REP * P + P], eye16)
                last.then_inc(turned[l][u].sem, 1)
                w[0].lend(kT_ready[l][u], 1)

            def attend(it, l, u):
                for event in (qT_a, qT_b, kT_ready):
                    pe.wait_ge(event[l][u].sem, event[l][u].at(it, 1))

                def score(n):
                    g = first[l, u] + n
                    pe.wait_ge(exped.sem, exped.at(it, max(g - 1, 0)))
                    if l == 0:
                        kt, c, js, width, step = groups1(n)
                        for h, j in enumerate(js):
                            last = nc.tensor.matmul(ps_s[:, g % 2, step * h:step * h + width],
                                                    kT[u][:, j, PAD + P * kt:PAD + P * kt + P],
                                                    qT[u][:, c, P * kt:S], start=True, stop=True)
                    else:
                        for j in range(KVH):
                            nc.tensor.matmul(ps_s[:, g % 2, 256 * j:256 * j + 256], eye16, window_sb[:, 0:REP * BLK],
                                             start=True, stop=False)
                            last = nc.tensor.matmul(ps_s[:, g % 2, 256 * j:256 * j + 256],
                                                    kT[u][:, j, BLK * n:BLK * n + P],
                                                    qT[u][:, :, BLK * n:BLK * n + BLK], start=False, stop=True)
                    last.then_inc(scores.sem, 1)

                def value(n):
                    g = first[l, u] + n
                    p = probs[g % PN]
                    if l == 0:
                        pe.wait_ge(masked[u].sem, masked[u].at(it, n + 1))
                        kt, c, js, width, step = groups1(n)
                        if n % 12 == 0:
                            o[c // 2].wait_free(pe, it)
                        for h, j in enumerate(js):
                            last = nc.tensor.matmul(ps_o[32 * j:32 * j + HW, c // 2, P * kt:S], v1[u][:, kt, j, c % 2, :],
                                                    p[:, step * h:step * h + width],
                                                    start=(kt == 0 and c % 2 == 0), stop=(kt == QT - 1 and c % 2 == 1),
                                                    skip_group_check=True)
                        if n % 12 == 11:
                            o[c // 2].lend(o_out[0][u], c // 2 + 1)
                    else:
                        pe.wait_ge(exped.sem, exped.at(it, g + 1))
                        t = n // 2
                        if n % 2 == 0:
                            o[t % 2].wait_free(pe, it)
                        for j in range(KVH):
                            last = nc.tensor.matmul(ps_o[32 * j:32 * j + HW, t % 2, 256 * (n % 2):256 * (n % 2) + 256],
                                                    v2[u][:, n, j, :], p[:, 256 * j:256 * j + 256], start=True, stop=True,
                                                    skip_group_check=True)
                        if n % 2 == 1:
                            o[t % 2].lend(o_out[1][u], t + 1)
                    last.then_inc(pv.sem, 1)

                count = GROUPS[l]
                for n in range(count + LAG):
                    if n < count:
                        score(n)
                    if n == LAG:
                        pe.wait_ge(v_ready[l][u].sem, v_ready[l][u].at(it, 1))
                    if n >= LAG:
                        value(n - LAG)

            def finish(it, l, u):
                if l == 0:
                    for n in range(2):
                        pe.wait_ge(o_out[0][u].sem, o_out[0][u].at(it, 2))
                        w[n].wait_free(pe, it)
                        for t in range(2):
                            for cb in range(2):
                                last = nc.tensor.transpose(ps_w[:, n, 256 * t + P * cb:256 * t + P * cb + P],
                                                           o_sb[cb][:, P * (2 * n + t):P * (2 * n + t) + P], eye_sb[:, :])
                        last.then_inc(o_turned[0][u].sem, 1)
                        w[n].lend(on_part[0][u], n + 1)
                else:
                    for t in range(QT):
                        pe.wait_ge(o_out[1][u].sem, o_out[1][u].at(it, t + 1))
                        w[t % 2].wait_free(pe, it)
                        for c in range(REP):
                            last = nc.tensor.transpose(ps_w[:, t % 2, P * c:P * c + P], o_sb[t % 2][:, P * c:P * c + P], eye_sb[:, :])
                        last.then_inc(o_turned[1][u].sem, 1)
                        w[t % 2].lend(on_part[1][u], t + 1)
                pe.wait_ge(on_part[l][u].sem, on_part[l][u].at(it, (2, 4)[l]))
                w[0].wait_free(pe, it)
                for t in range(QT):
                    last = nc.tensor.transpose(ps_w[:, 0, P * t:P * t + P], on[:, t, :], eye_sb[:, :])
                last.then_inc(on_turned[l][u].sem, 1)
                w[0].lend(oT_ready[l][u], 1)
                pe.wait_ge(oT_ready[l][u].sem, oT_ready[l][u].at(it, 1))
                w[1].wait_free(pe, it)
                for t in range(QT):
                    last = nc.tensor.matmul(ps_w[:, 1, P * t:P * t + P], oT[:, P * t:P * t + P], wo_sb[:, l, :], start=True, stop=True)
                last.then_inc(proj_ready[l][u].sem, 1)
                w[1].lend((x2_ready, z_ready)[l][u], 1)

            def route(it, u):
                pe.wait_ge(x1_ready[u].sem, x1_ready[u].at(it, 1))
                w[0].wait_free(pe, it)
                for t in range(QT):
                    last = nc.tensor.transpose(ps_w[:, 0, P * t:P * t + P], x1[u][:, t, 0:D], eye_sb[:, :])
                last.then_inc(x1_turned[u].sem, 1)
                w[0].lend(x1T_ready[u], 1)
                pe.wait_ge(x1T_ready[u].sem, x1T_ready[u].at(it, 1))
                w[1].wait_free(pe, it)
                for t in range(QT):
                    last = nc.tensor.matmul(ps_w[:, 1, E * t:E * t + E], x1T[:, P * t:P * t + P], router_sb[:, :], start=True, stop=True)
                last.then_inc(logits_ready[u].sem, 1)
                w[1].lend(logits_out[u], 1)
                pe.wait_ge(sel_ready[u].sem, sel_ready[u].at(it, 1))
                w[0].wait_free(pe, it)
                chosen = sel16[:, :, :].rearrange("p t e -> p (t e)")
                nc.tensor.matmul(ps_w[:, 0, 0:QT * E], before16, chosen, start=True, stop=True)
                nc.tensor.matmul(ps_w[:, 0, 64:64 + QT * E], ones16, chosen, start=True, stop=True).then_inc(ranks_ready[u].sem, 1)
                w[0].lend(ranks_out[u], 1)

            pe.wait_ge(weights_ready, 3)
            pe.wait_ge(loaded["attn"], 16 * ATTN_LOADS)
            pe.sem_inc(pv.sem, 1)
            with pe.Fori(0, PASSES) as it:
                project(it, 0, 0)
                turn_heads(it, 0, 0)
                project(it, 0, 1)
                turn_heads(it, 0, 1)
                attend(it, 0, 0)
                finish(it, 0, 0)
                turn_x2(it, 0)
                project(it, 1, 0)
                turn_heads(it, 1, 0)
                attend(it, 0, 1)
                finish(it, 0, 1)
                turn_x2(it, 1)
                project(it, 1, 1)
                turn_heads(it, 1, 1)
                attend(it, 1, 0)
                finish(it, 1, 0)
                route(it, 0)
                attend(it, 1, 1)
                finish(it, 1, 1)
                route(it, 1)

            pe.wait_ge(wsum_ready, 1)
            nc.tensor.matmul(ps_w[:, 1, 0:E], ones_sb[:, :], c_f[3][:, :], start=True, stop=True).then_inc(counted, 1)

            def turn_rows(i, n, pair):
                pe.wait_ge(xs_loaded[n], 16 * (pair + 1))
                pe.wait_ge(xsT_ready, i)
                nc.tensor.transpose(ps_w[:, 0, 0:P], xs[n][:, 0:D], eye_sb[:, :]).then_inc(xs_turned, 1)

            def gate_up(i, n):
                e = pe.value_load(te_sb[0:1, bass.ds(i, 1)], min_val=0, max_val=E - 1)
                pe.wait_ge(xsT_ready, i + 1)
                nc.tensor.matmul(ps_s[:, n, 0:F], xsT[n][:, :], gate_sb[:, bass.ds(e * F, F)], start=True, stop=True)
                nc.tensor.matmul(ps_s[:, n, F:2 * F], xsT[n][:, :], up_sb[:, bass.ds(e * F, F)], start=True, stop=True).then_inc(gu_ready, 1)

            def turn_hidden(i, n):
                pe.wait_ge(hid_ready, i + 1)
                for f in range(FC):
                    last = nc.tensor.transpose(ps_o[:, n, P * f:P * f + P], hid[n][:, P * f:P * f + P], eye_sb[:, :])
                last.then_inc(hid_turned, 1)

            def down(i, n, first=False):
                e = pe.value_load(te_sb[0:1, bass.ds(i, 1)], min_val=0, max_val=E - 1)
                pe.wait_ge(hT_ready, i + 1)
                if not first:
                    pe.wait_ge(ys_ready, i)
                for f in range(FC):
                    last = nc.tensor.matmul(ps_w[:, 1, 0:D], hT[n][:, P * f:P * f + P],
                                            mlp_down_sb[:, bass.ds(e * (FC * D) + f * D, D)], start=(f == 0), stop=(f == FC - 1))
                last.then_inc(y_ready, 1)

            pe.wait_ge(tables, 3)
            pe.wait_ge(loaded["mlp"], 48)
            pe.wait_ge(xs_loaded[0], 16)
            nc.tensor.transpose(ps_w[:, 0, 0:P], xs[0][:, 0:D], eye_sb[:, :]).then_inc(xs_turned, 1)
            gate_up(0, 0)
            turn_rows(1, 1, 0)

            def tile_pair(k, first=False):
                for n in range(2):
                    turn_hidden(2 * k + n, n)
                    gate_up(2 * k + (n + 1), 1 - n)
                    turn_rows(2 * k + (n + 2), n, k + 1)
                    down(2 * k + n, n, first and n == 0)

            tile_pair(0, first=True)
            with pe.Fori(1, (TILES - 1) // 2) as k:
                tile_pair(k)
            turn_hidden(TILES - 1, 0)
            down(TILES - 1, 0)

        @block.scalar
        def _(act):
            for dst, src in ((wo_sb[:, :, :], wo.rearrange("p (l n) -> p l n", l=2)), (window_sb[:, :], window),
                             (expert_sb[:, :], expert), (ids_sb[:, :], ids), (router_sb[:, :], router_t),
                             (ones_sb[:, :], ones), (tile_no_sb[:, :, :], tile_no.rearrange("p (t e) -> p t e", e=E))):
                act.dma_start(dst, src).then_inc(loaded["attn"], 16)
            act.wait_ge(loaded["attn"], 16 * ATTN_LOADS)

            def squares(it, l, u):
                if l == 0:
                    act.wait_ge(x_loaded[u].sem, x_loaded[u].at(it, 32))
                    act.wait_ge(arg_ready[0][u].sem, arg_ready[0][u].at(it, 0))
                    src = x_in[u]
                else:
                    act.wait_ge(x2_ready[u].sem, x2_ready[u].at(it, 1))
                    src = x2[u]
                nc.scalar.activation(xsq[u][:, :, :], src[:, :, :], ACT.Square).then_inc(sq_ready[l][u].sem, 1)

            def copy_x2(it, u):
                act.wait_ge(x2_turned[u].sem, x2_turned[u].at(it, 1))
                nc.scalar.copy(xT[u][:, :], ps_w[:, 0, :]).then_inc(x2T_ready[u].sem, 1)

            def copy_raw(it, l, u):
                act.wait_ge(split_ready[l][u].sem, split_ready[l][u].at(it, 0))
                act.wait_ge(v_ready[l][u].sem, v_ready[l][u].at(it, 0))
                for n in range(2):
                    act.wait_ge(qkv_ready[l][u].sem, qkv_ready[l][u].at(it, n + 1))
                    src = ps_w[:, n, :].rearrange("p (t n) -> p t n", t=2)[:, :, 0:QKV]
                    nc.scalar.copy(raw[u][:, 2 * n:2 * n + 2, :], src).then_inc(raw_ready[l][u].sem, 1)
                act.wait_ge(raw_ready[l][u].sem, raw_ready[l][u].at(it, 2))
                nc.scalar.activation(sq[u][:, :, :], raw[u][:, :, 0:NH * HD], ACT.Square).then_inc(sq_ready[l][u].sem, 1)

            def guess_root(it, l, u):
                act.wait_ge(arg_ready[l][u].sem, arg_ready[l][u].at(it, 1))
                nc.scalar.activation(inv[u][:, :, :], ms[u][:, :, :], ACT.Ln).then_inc(ln_ready[l][u].sem, 1)
                act.wait_ge(ln_ready[l][u].sem, ln_ready[l][u].at(it, 1))
                nc.scalar.activation(inv[u][:, :, :], inv[u][:, :, :], ACT.Exp, scale=-0.5).then_inc(guess_ready[l][u].sem, 1)

            def copy_queries(it, l, u):
                act.wait_ge(turned[l][u].sem, turned[l][u].at(it, 2))
                src = ps_w[:, 1, :].bitcast(F16).rearrange("p (c n) -> p c n", c=REP)
                nc.scalar.copy(qT[u][:, :, 256:512], src).then_inc(qT_b[l][u].sem, 1)

            def exponentials(it, l, u):
                for n in range(GROUPS[l]):
                    g = first[l, u] + n
                    act.wait_ge(scores.sem, scores.at(it, g + 1))
                    act.wait_ge(pv.sem, pv.at(it, max(g - PN + 1, 0)))
                    if l == 0:
                        kt, c, js, width, step = groups1(n)
                    else:
                        js, width, step = range(2), 512, 512
                    src = ps_s[:, g % 2, 0:len(js) * step].rearrange("p (h n) -> p h n", n=step)[:, :, 0:width]
                    nc.scalar.activation(prob_heads(g, len(js), step, width), src, ACT.Exp, scale=SCALE).then_inc(exped.sem, 1)

            def copy_outputs(it, l, u):
                act.wait_ge(on_turned[l][u].sem, on_turned[l][u].at(it, 1))
                nc.scalar.copy(oT[:, :], ps_w[:, 0, :]).then_inc(oT_ready[l][u].sem, 1)

            def norm_and_route(it, u):
                act.wait_ge(zc_ready[u].sem, zc_ready[u].at(it, 1))
                nc.scalar.activation(z[:, :, :], zc[:, :, :], ACT.Square).then_inc(zsq_ready[u].sem, 1)
                act.wait_ge(zarg_ready[u].sem, zarg_ready[u].at(it, 1))
                nc.scalar.activation(ln_s[:, 3, :], ln_s[:, 2, :], ACT.Ln).then_inc(zln_ready[u].sem, 1)
                act.wait_ge(zln_ready[u].sem, zln_ready[u].at(it, 1))
                nc.scalar.activation(ln_s[:, 3, :], ln_s[:, 3, :], ACT.Exp, scale=-0.5).then_inc(zguess_ready[u].sem, 1)
                act.wait_ge(x1_turned[u].sem, x1_turned[u].at(it, 1))
                nc.scalar.copy(x1T[:, :], ps_w[:, 0, :]).then_inc(x1T_ready[u].sem, 1)
                act.wait_ge(gap_ready[u].sem, gap_ready[u].at(it, 1))
                nc.scalar.activation(r_s[:, 5, :], r_s[:, 4, :], ACT.Exp).then_inc(ratio_ready[u].sem, 1)

            def prepare(it, l, u):
                squares(it, l, u)
                if l == 1:
                    copy_x2(it, u)
                copy_raw(it, l, u)
                guess_root(it, l, u)
                copy_queries(it, l, u)

            act.sem_inc(exped.sem, 1)
            with act.Fori(0, PASSES) as it:
                prepare(it, 0, 0)
                prepare(it, 0, 1)
                exponentials(it, 0, 0)
                copy_outputs(it, 0, 0)
                prepare(it, 1, 0)
                exponentials(it, 0, 1)
                copy_outputs(it, 0, 1)
                prepare(it, 1, 1)
                exponentials(it, 1, 0)
                copy_outputs(it, 1, 0)
                norm_and_route(it, 0)
                exponentials(it, 1, 1)
                copy_outputs(it, 1, 1)
                norm_and_route(it, 1)

            def silu(i, n):
                act.wait_ge(gu_ready, i + 1)
                nc.scalar.activation(sg[n], ps_s[:, n, 0:F], ACT.Silu).then_inc(silu_ready, 1)

            act.wait_ge(xs_turned, 1)
            nc.scalar.copy(xsT[0][:, :], ps_w[:, 0, 0:P]).then_inc(xsT_ready, 1)
            act.wait_ge(xs_turned, 2)
            nc.scalar.copy(xsT[1][:, :], ps_w[:, 0, 0:P]).then_inc(xsT_ready, 1)
            with act.Fori(0, (TILES - 1) // 2) as k:
                for n in range(2):
                    i = 2 * k + n
                    silu(i, n)
                    act.wait_ge(xs_turned, i + 3)
                    nc.scalar.copy(xsT[n][:, :], ps_w[:, 0, 0:P]).then_inc(xsT_ready, 1)
            silu(TILES - 1, 0)

            for b in range(B):
                act.wait_ge(fin_c, b + 1)
                nc.scalar.activation(fin_z[b][0][:, :, :], fin_z[b][1][:, :, :], ACT.Square).then_inc(fin_sq, 1)
                act.wait_ge(fin_arg, b + 1)
                nc.scalar.activation(c_r[0][:, 4 * b:4 * b + 4], c_r[1][:, 4 * b:4 * b + 4], ACT.Ln).then_inc(act_own, 1)
                act.wait_ge(act_own, b + 1)
                nc.scalar.activation(c_r[0][:, 4 * b:4 * b + 4], c_r[0][:, 4 * b:4 * b + 4], ACT.Exp, scale=-0.5).then_inc(fin_guess, 1)

        @block.vector
        def _(dve):
            dve.wait_ge(loaded["consts"], 16 * CONSTS)
            dve.wait_ge(loaded["attn"], 16 * ATTN_LOADS)
            own = Chain(dve, dve_own)
            own.do(nc.vector.memset(pad_rows[:, :], 0.0))
            for u in range(HALVES):
                own.do(nc.vector.memset(x1[u][:, :, D:ROW], 0.0))
            own.do(nc.vector.memset(wacc[:, :, :], 0.0))
            own.do(nc.vector.tensor_copy(run[:, 0, :], expert_sb[:, 0:E]))
            nc.vector.tensor_scalar(wqkv[:, 0, 0:D], wq1[:, :], norm_sb[:, 0:1], None, ALU.mult).then_inc(weights_ready, 1)
            nc.vector.tensor_scalar(wqkv[:, 1, :], wraw2[:, :], norm_sb[:, 1:2], None, ALU.mult).then_inc(weights_ready, 1)
            dve.wait_ge(fold_ready, 1)
            nc.vector.tensor_scalar(wqkv[:, 0, D:QKV], ps_w[:, 0, 0:QKV - D], norm_sb[:, 0:1], None, ALU.mult).then_inc(weights_ready, 1)
            own.sync()
            nc.vector.tensor_copy(pad_rows[:, D:D + 1], expert_sb[:, 2 * E:2 * E + 1]).then_inc(pad_set, 1)
            before_loop = own.n
            dve.wait_ge(pool_own, 14)

            def inverse_root(chain, y, v, a, b):
                chain.step(nc.vector.scalar_tensor_tensor(out=a, in0=y, scalar=-0.5, in1=v, op0=ALU.mult, op1=ALU.mult))
                chain.step(nc.vector.tensor_tensor(b, a, y, ALU.mult))
                return nc.vector.scalar_tensor_tensor(out=y, in0=b, scalar=1.5, in1=y, op0=ALU.add, op1=ALU.mult)

            def mean_squares(chain, it, l, u):
                dve.wait_ge(sq_ready[l][u].sem, sq_ready[l][u].at(it, 2))
                chain.do(nc.vector.tensor_reduce(ms[u][:, :, NH:NH + 1], xsq[u][:, :, :], AX.X, ALU.add))
                chain.step(nc.vector.tensor_reduce(ms[u][:, :, 0:NH], sq[u][:, :, :].rearrange("p t (h d) -> p t h d", d=HD), AX.X, ALU.add))
                x_ms = ms[u][:, :, NH:NH + 1]
                chain.step(nc.vector.tensor_scalar(x_ms, x_ms, 1.0 / D, RMS_EPS, ALU.mult, ALU.add))
                small = t_b[:, 0:QT].rearrange("p (t o) -> p t o", o=1)
                chain.step(nc.vector.tensor_scalar(small, x_ms, RMS_EPS, None, ALU.mult))
                tell(dve, nc.vector.scalar_tensor_tensor(out=ms[u][:, :, 0:NH], in0=ms[u][:, :, 0:NH], scalar=1.0 / HD,
                                                         in1=small.broadcast_to((P, QT, NH)), op0=ALU.mult, op1=ALU.add),
                     arg_ready[l][u], it, 1)

            def rotate(chain, it, l, u):
                dve.wait_ge(guess_ready[l][u].sem, guess_ready[l][u].at(it, 1))
                a3, b3 = (t[:, :].rearrange("p (t h) -> p t h", t=QT) for t in (t_a, t_b))
                tell(dve, inverse_root(chain, inv[u][:, :, :], ms[u][:, :, :], a3, b3), inv_ready[l][u], it, 1)
                root = inv[u][:, :, 0:NH].unsqueeze(3).broadcast_to((P, QT, NH, HD))
                chain.step(nc.vector.tensor_tensor(qn[:, :, :, :], raw[u][:, :, 0:NH * HD].rearrange("p t (h d) -> p t h d", d=HD), root, ALU.mult))
                val = raw[u][:, :, NH * HD:QKV].rearrange("p t (j d) -> p t j d", d=HD)
                row = inv[u][:, :, NH:NH + 1].unsqueeze(3).broadcast_to((P, QT, KVH, HD))
                if l == 0:
                    chain.do(nc.vector.tensor_tensor(v1[u][:, :, :, 0, 0:HD], val, row, ALU.mult))
                    nc.vector.tensor_tensor(v1[u][:, :, :, 1, 2 * HD:3 * HD], val, row, ALU.mult).then_inc(v_ready[0][u].sem, 1)
                else:
                    pairs = v2[u][:, :, :, :].rearrange("p (t o) j d -> p t o j d", o=2)
                    chain.step(nc.vector.tensor_tensor(pairs[:, :, 1, :, 0:HD], val, row, ALU.mult))
                    chain.do(nc.vector.tensor_copy(pairs[BLK:P, :, 0, :, 0:HD], pairs[0:BLK, :, 1, :, 0:HD]))
                    nc.vector.tensor_copy(pairs[0:BLK, 1:QT, 0, :, 0:HD], pairs[BLK:P, 0:QT - 1, 1, :, 0:HD]).then_inc(v_ready[1][u].sem, 1)
                half_heads = "p t h (o f) -> p t (h o) f"
                cos, sin = (rope_sb[:, l, n, :, :].unsqueeze(2).broadcast_to((P, QT, 2 * NH, HD // 2)) for n in range(2))
                q4 = qn[:, :, :, :].rearrange(half_heads, o=2)
                chain.do(nc.vector.tensor_tensor(by_cos[:, :, :, :].rearrange(half_heads, o=2), q4, cos, ALU.mult))
                chain.step(nc.vector.tensor_tensor(by_sin[:, :, :, :].rearrange(half_heads, o=2), q4, sin, ALU.mult))
                lo, hi = slice(0, HD // 2), slice(HD // 2, HD)
                chain.do(nc.vector.tensor_tensor(rot[:, :, :, lo], by_cos[:, :, :, lo], by_sin[:, :, :, hi], ALU.subtract))
                chain.step(nc.vector.tensor_tensor(rot[:, :, :, hi], by_sin[:, :, :, lo], by_cos[:, :, :, hi], ALU.add))
                x16 = qk16[u]
                chain.step(nc.vector.tensor_copy(x16[:, :, :, 0, :], rot[:, :, :, :]))
                chain.step(nc.vector.tensor_tensor(x16[:, :, :, 3, :], rot[:, :, :, :], x16[:, :, :, 0, :], ALU.subtract))
                for dst, src in ((1, 3), (2, 0)):
                    chain.do(nc.vector.tensor_copy(x16[:, :, 0:H, dst, :], x16[:, :, 0:H, src, :]))
                chain.do(nc.vector.tensor_copy(x16[:, :, H:NH, 1, :], x16[:, :, H:NH, 0, :]))
                tell(dve, nc.vector.tensor_copy(x16[:, :, H:NH, 2, :], x16[:, :, H:NH, 3, :]), split_ready[l][u], it, 1)

            def copy_heads(chain, it, l, u):
                dve.wait_ge(turned[l][u].sem, turned[l][u].at(it, 1))
                src = ps_w[:, 0, :].bitcast(F16).rearrange("p (c n) -> p c n", c=REP)
                nc.vector.tensor_copy(qT[u][:, :, 0:256], src).then_inc(qT_a[l][u].sem, 1)
                dve.wait_ge(turned[l][u].sem, turned[l][u].at(it, 3))
                for j in range(KVH):
                    rows_j = slice(HW * j, HW * j + HW)
                    last = nc.vector.tensor_copy(kT[u][rows_j, j, PAD:PAD + S], ps_w[rows_j, 0, :].bitcast(F16)[:, 0:S])
                    if j < KVH - 1:
                        chain.do(last)
                last.then_inc(kT_ready[l][u].sem, 1)

            def normalise(chain, it, l, u):
                if l == 0:
                    for cb in range(2):
                        dve.wait_ge(pv.sem, pv.at(it, first[0, u] + 12 * (cb + 1)))
                        tell(dve, nc.vector.tensor_copy(o_sb[cb][:, :], ps_o[:, cb, :]), o_out[0][u], it, cb + 1)
                    for n in range(2):
                        dve.wait_ge(o_turned[0][u].sem, o_turned[0][u].at(it, n + 1))
                        heads = ps_w[:, n, :].rearrange("p (a h) -> p a h", h=2 * HD)
                        den = rden[:, 0:4 * HD].rearrange("p (a o) -> p a o", o=1)
                        chain.step(nc.vector.reciprocal(den, heads[:, :, HD:HD + 1]))
                        dst = on[:, 2 * n:2 * n + 2, :].rearrange("p t (a d) -> p (t a) d", d=HD)
                        tell(dve, nc.vector.tensor_tensor(dst, heads[:, :, 0:HD], den.broadcast_to((P, 4 * HD, HD)), ALU.mult), on_part[0][u], it, n + 1)
                else:
                    def copy_out(t):
                        dve.wait_ge(pv.sem, pv.at(it, first[1, u] + 2 * (t + 1)))
                        src = ps_o[:, t % 2, :].rearrange("p (m c q) -> p m c q", m=2, c=REP)
                        dst = o_sb[t % 2][:, :].rearrange("p (c m q) -> p m c q", m=2, c=REP)
                        tell(dve, nc.vector.tensor_copy(dst, src), o_out[1][u], it, t + 1)

                    copy_out(0)
                    for t in range(QT):
                        if t + 1 < QT:
                            copy_out(t + 1)
                        dve.wait_ge(o_turned[1][u].sem, o_turned[1][u].at(it, t + 1))
                        heads = ps_w[:, t % 2, :].rearrange("p (a h) -> p a h", h=HW)
                        den = rden[:, 0:H].rearrange("p (a o) -> p a o", o=1)
                        chain.step(nc.vector.reciprocal(den, heads[:, :, HD:HD + 1]))
                        dst = on[:, t, :].rearrange("p (a d) -> p a d", d=HD)
                        tell(dve, nc.vector.tensor_tensor(dst, heads[:, :, 0:HD], den.broadcast_to((P, H, HD)), ALU.mult), on_part[1][u], it, t + 1)

            def residual1(chain, it, u):
                dve.wait_ge(proj_ready[0][u].sem, proj_ready[0][u].at(it, 1))
                src = ps_w[:, 1, :].rearrange("p (t d) -> p t d", d=D)
                tell(dve, nc.vector.tensor_tensor(x2[u][:, :, :], src, x_in[u][:, :, :], ALU.add), x2_ready[u], it, 1)

            def residual2(chain, it, u):
                dve.wait_ge(proj_ready[1][u].sem, proj_ready[1][u].at(it, 1))
                src = ps_w[:, 1, :].rearrange("p (t d) -> p t d", d=D)
                tell(dve, nc.vector.tensor_tensor(z[:, :, :], src, x2[u][:, :, :], ALU.add), z_ready[u], it, 1)
                chain.step(nc.vector.tensor_tensor(z[:, :, :], z[:, :, :], x_in[u][:, :, :], ALU.add))
                total, mean, var, root = (ln_s[:, n, :].rearrange("p (t o) -> p t o", o=1) for n in range(4))
                chain.step(nc.vector.tensor_reduce(total, z[:, :, :], AX.X, ALU.add))
                chain.step(nc.vector.tensor_scalar(mean, total, 1.0 / D, None, ALU.mult))
                tell(dve, nc.vector.tensor_tensor(zc[:, :, :], z[:, :, :], mean.broadcast_to((P, QT, D)), ALU.subtract), zc_ready[u], it, 1)
                dve.wait_ge(zsq_ready[u].sem, zsq_ready[u].at(it, 1))
                chain.step(nc.vector.tensor_reduce(var, z[:, :, :], AX.X, ALU.add))
                tell(dve, nc.vector.tensor_scalar(var, var, 1.0 / D, LN_EPS, ALU.mult, ALU.add), zarg_ready[u], it, 1)
                dve.wait_ge(zguess_ready[u].sem, zguess_ready[u].at(it, 1))
                a3, b3 = (t[:, 0:QT].rearrange("p (t o) -> p t o", o=1) for t in (t_a, t_b))
                chain.step(inverse_root(chain, root, var, a3, b3))
                dve.wait_ge(x1_free[u].sem, x1_free[u].at(it, 0))
                ids_now = ids_sb[:, bass.ds((it * HALVES + u) * QT, QT)].rearrange("p (t o) -> p t o", o=1)
                chain.do(nc.vector.tensor_copy(x1[u][:, :, D:D + 1], ids_now))
                chain.sync()
                tell(dve, nc.vector.tensor_tensor(x1[u][:, :, 0:D], zc[:, :, :], root.broadcast_to((P, QT, D)), ALU.mult), x1_ready[u], it, 1)

            def choose(chain, it, u):
                dve.wait_ge(logits_ready[u].sem, logits_ready[u].at(it, 1))
                tell(dve, nc.vector.tensor_copy(lg[:, :, :], ps_w[:, 1, 0:QT * E].rearrange("p (t e) -> p t e", e=E)), logits_out[u], it, 1)
                order = expert_sb[:, E:2 * E].unsqueeze(1).broadcast_to((P, QT, E))
                s3 = [r_s[:, n, :].rearrange("p (t o) -> p t o", o=1) for n in range(8)]
                wide = [s.broadcast_to((P, QT, E)) for s in s3]
                src = lg
                for k in range(2):
                    chain.step(nc.vector.tensor_reduce(s3[k], src[:, :, :], AX.X, ALU.max))
                    chain.step(nc.vector.tensor_tensor(r_t[0][:, :, :], src[:, :, :], wide[k], ALU.is_ge))
                    chain.step(nc.vector.tensor_tensor(r_t[1][:, :, :], r_t[0][:, :, :], order, ALU.mult))
                    chain.step(nc.vector.tensor_reduce(s3[2 + k], r_t[1][:, :, :], AX.X, ALU.max))
                    chain.step(nc.vector.tensor_tensor(sel[k][:, :, :], r_t[1][:, :, :], wide[2 + k], ALU.is_equal))
                    if k == 0:
                        chain.step(nc.vector.scalar_tensor_tensor(out=r_t[2][:, :, :], in0=sel[0][:, :, :], scalar=-3e38,
                                                                  in1=lg[:, :, :], op0=ALU.mult, op1=ALU.add))
                        src = r_t[2]
                tell(dve, nc.vector.tensor_tensor(s3[4], s3[1], s3[0], ALU.subtract), gap_ready[u], it, 1)
                tell(dve, nc.vector.tensor_tensor(sel16[:, :, :], sel[0][:, :, :], sel[1][:, :, :], ALU.add), sel_ready[u], it, 1)
                dve.wait_ge(ratio_ready[u].sem, ratio_ready[u].at(it, 1))
                chain.step(nc.vector.tensor_scalar(s3[6], s3[5], 1.0, None, ALU.add))
                chain.step(nc.vector.reciprocal(s3[6], s3[6]))
                chain.step(nc.vector.tensor_tensor(s3[7], s3[5], s3[6], ALU.mult))
                for k in range(2):
                    chain.step(nc.vector.tensor_tensor(r_t[k][:, :, :], sel[k][:, :, :], wide[6 + k], ALU.mult))
                    chain.step(nc.vector.tensor_tensor(wacc[:, :, :], wacc[:, :, :], r_t[k][:, :, :], ALU.add))
                dve.wait_ge(ranks_ready[u].sem, ranks_ready[u].at(it, 1))
                for t in range(QT):
                    chain.step(nc.vector.tensor_tensor(run[:, t + 1, :], run[:, t, :], ps_w[:, 0, 64 + E * t:64 + E * t + E], ALU.add))
                tell(dve, nc.vector.tensor_tensor(r_t[3][:, :, :], run[:, 0:QT, :], ps_w[:, 0, 0:QT * E].rearrange("p (t e) -> p t e", e=E), ALU.add),
                     ranks_out[u], it, 1)
                chain.do(nc.vector.tensor_copy(run[:, 0, :], run[:, QT, :]))
                for k in range(2):
                    chain.step(nc.vector.tensor_tensor(r_t[k][:, :, :], sel[k][:, :, :], r_t[3][:, :, :], ALU.mult))
                    chain.step(nc.vector.tensor_reduce(s3[k], r_t[k][:, :, :], AX.X, ALU.add))
                both = r_s[:, 0:2, :]
                tell(dve, nc.vector.tensor_copy(slot[u][:, :, :], both), slots_ready[u], it, 1)

            for u in range(HALVES):
                for event in (arg_ready[0][u], v_ready[0][u], split_ready[0][u], o_out[0][u], x1_ready[u], logits_out[u], ranks_out[u]):
                    dve.sem_inc(event.sem, 1)
            with dve.Fori(0, PASSES) as it:
                chain = Chain(dve, dve_own, it, DVE_STEPS, before_loop)

                def prepare(l, u):
                    mean_squares(chain, it, l, u)
                    rotate(chain, it, l, u)
                    copy_heads(chain, it, l, u)

                prepare(0, 0)
                prepare(0, 1)
                normalise(chain, it, 0, 0)
                residual1(chain, it, 0)
                prepare(1, 0)
                normalise(chain, it, 0, 1)
                residual1(chain, it, 1)
                prepare(1, 1)
                normalise(chain, it, 1, 0)
                residual2(chain, it, 0)
                choose(chain, it, 0)
                normalise(chain, it, 1, 1)
                residual2(chain, it, 1)
                choose(chain, it, 1)
                assert chain.n == DVE_STEPS, chain.n

            own = Chain(dve, dve_own, 0, 0, before_loop + PASSES * DVE_STEPS)
            own.do(nc.vector.tensor_reduce(c_f[3][:, :], wacc[:, :, :].rearrange("p t e -> p e t"), AX.X, ALU.add))
            own.sync()
            nc.vector.tensor_copy(c_f[2][:, :], c_f[3][:, :]).then_inc(wsum_ready, 1)
            count, tiles, starts = c_f[0], c_f[1], c_f[2]
            base = expert_sb[:, 0:E]
            nc.vector.tensor_copy(end_sb[:, :], run[:, 0, :]).then_inc(tables, 1)
            own.step(nc.vector.tensor_tensor(count[:, :], run[:, 0, :], base, ALU.subtract))
            own.step(nc.vector.tensor_scalar(c_i[:, :], count[:, :], float(P - 1), None, ALU.add))
            own.step(nc.vector.tensor_scalar(c_i[:, :], c_i[:, :], 7, None, ALU.arith_shift_right))
            own.step(nc.vector.tensor_copy(tiles[:, :], c_i[:, :]))
            ends = c_t[0][:, 0, :]
            own.step(nc.vector.tensor_copy(ends[:, 0:1], tiles[:, 0:1]))
            for e in range(1, E):
                own.step(nc.vector.tensor_tensor(ends[:, e:e + 1], ends[:, e - 1:e], tiles[:, e:e + 1], ALU.add))
            dve.wait_ge(wsum_ready, 1)
            own.step(nc.vector.tensor_tensor(starts[:, :], ends, tiles[:, :], ALU.subtract))
            own.do(nc.vector.tensor_tensor(c_t[1][:, :, :], tile_no_sb[:, :, :], ends.unsqueeze(1).broadcast_to((P, TILES, E)), ALU.is_ge))
            own.step(nc.vector.tensor_tensor(c_t[2][:, :, :], tile_no_sb[:, :, :], starts[:, :].unsqueeze(1).broadcast_to((P, TILES, E)), ALU.is_ge))
            own.do(nc.vector.tensor_reduce(c_r[0][:, 0:TILES], c_t[1][:, :, :], AX.X, ALU.add))
            own.do(nc.vector.tensor_scalar(starts[:, :], starts[:, :], -float(P), None, ALU.mult))
            own.sync()
            own.do(nc.vector.tensor_tensor(starts[:, :], starts[:, :], base, ALU.add))
            own.step(nc.vector.tensor_tensor(c_t[2][:, :, :], c_t[2][:, :, :], c_t[1][:, :, :], ALU.subtract))
            own.step(nc.vector.scalar_tensor_tensor(out=c_t[0][:, :, :], in0=tile_no_sb[:, :, :], scalar=float(P),
                                                    in1=starts[:, :].unsqueeze(1).broadcast_to((P, TILES, E)), op0=ALU.mult, op1=ALU.add))
            own.step(nc.vector.tensor_tensor(c_t[0][:, :, :], c_t[0][:, :, :], c_t[2][:, :, :], ALU.mult))
            own.do(nc.vector.tensor_reduce(c_r[1][:, 0:TILES], c_t[0][:, :, :], AX.X, ALU.add))
            own.step(nc.vector.memset(c_r[1][:, TILES:TILES + 1], float(PADROW)))
            past = c_t[1][:, :, E - 1]
            own.step(nc.vector.scalar_tensor_tensor(out=c_r[1][:, 0:TILES], in0=past, scalar=float(PADROW), in1=c_r[1][:, 0:TILES], op0=ALU.mult, op1=ALU.add))
            nc.vector.tensor_copy(row_sb[:, :], c_r[1][:, :]).then_inc(tables, 1)
            own.step(nc.vector.memset(c_r[0][:, TILES:TILES + 1], 0.0))
            own.step(nc.vector.tensor_scalar(c_r[0][:, :], c_r[0][:, :], float(E - 1), None, ALU.min))
            nc.vector.tensor_copy(te_sb[:, :], c_r[0][:, :]).then_inc(tables, 1)
            own.step(nc.vector.tensor_scalar(count[:, :], count[:, :], 1.0, None, ALU.max))
            own.step(nc.vector.reciprocal(count[:, :], count[:, :]))
            dve.wait_ge(counted, 1)
            own.step(nc.vector.tensor_tensor(mean_w[:, :], ps_w[:, 1, 0:E], count[:, :], ALU.mult))
            dve.wait_ge(tables, 3)

            def hidden(i, n):
                dve.wait_ge(silu_ready, i + 1)
                nc.vector.tensor_tensor(hid[n], sg[n], ps_s[:, n, F:2 * F], ALU.mult).then_inc(hid_ready, 1)

            def copy_hidden(i, n):
                dve.wait_ge(hid_turned, i + 1)
                nc.vector.tensor_copy(hT[n], ps_o[:, n, :]).then_inc(hT_ready, 1)

            def read_ids(n, pair):
                dve.wait_ge(xs_loaded[n], 16 * (pair + 1))
                nc.vector.tensor_copy(idu[n][:, :], xs[n][:, D:D + 1]).then_inc(idu_ready, 1)

            def weigh(i, n):
                e = dve.value_load(te_sb[0:1, bass.ds(i, 1)], min_val=0, max_val=E - 1)
                dve.wait_ge(y_ready, i + 1)
                nc.vector.tensor_scalar(ys[n][:, :], ps_w[:, 1, 0:D], mean_w[:, bass.ds(e, 1)], None, ALU.mult).then_inc(ys_ready, 1)

            read_ids(0, 0)
            hidden(0, 0)
            read_ids(1, 0)

            def tile_pair(k, first=False):
                for n in range(2):
                    i = 2 * k + n
                    copy_hidden(i, n)
                    hidden(i + 1, 1 - n)
                    if not first:
                        dve.wait_ge(added, 16 * (i - 1))
                    weigh(i, n)
                    dve.wait_ge(added, 16 * (i + 1))
                    read_ids(n, k + 1)

            tile_pair(0, first=True)
            with dve.Fori(1, (TILES - 1) // 2) as k:
                tile_pair(k)
            copy_hidden(TILES - 1, 0)
            dve.wait_ge(added, 16 * (TILES - 2))
            weigh(TILES - 1, 0)

            own = Chain(dve, dve_own, 0, 0, before_loop + PASSES * DVE_STEPS + own.n)
            for b in range(B):
                src, cen = fin_z[b]
                dve.wait_ge(fin_loaded[b], 16)
                total, mean = (t[:, 8 * n:8 * n + QT].rearrange("p (t o) -> p t o", o=1) for n, t in enumerate((t_a, t_a)))
                var, root = (c_r[n][:, 4 * b:4 * b + 4].rearrange("p (t o) -> p t o", o=1) for n in (1, 0))
                own.step(nc.vector.tensor_reduce(total, src[:, :, :], AX.X, ALU.add))
                own.step(nc.vector.tensor_scalar(mean, total, 1.0 / D, None, ALU.mult))
                nc.vector.tensor_tensor(cen[:, :, :], src[:, :, :], mean.broadcast_to((P, QT, D)), ALU.subtract).then_inc(fin_c, 1)
                dve.wait_ge(fin_sq, b + 1)
                own.step(nc.vector.tensor_reduce(var, src[:, :, :], AX.X, ALU.add))
                nc.vector.tensor_scalar(var, var, 1.0 / D, LN_EPS, ALU.mult, ALU.add).then_inc(fin_arg, 1)
                dve.wait_ge(fin_guess, b + 1)
                a3, b3 = (t[:, 16:16 + QT].rearrange("p (t o) -> p t o", o=1) for t in (t_a, t_b))
                own.step(inverse_root(own, root, var, a3, b3))
                nc.vector.tensor_tensor(src[:, :, :], cen[:, :, :], root.broadcast_to((P, QT, D)), ALU.mult).then_inc(fin_ready, 1)


ATTN_LOADS = 7
CONSTS = 8
DVE_STEPS = 164


def kernel(**inputs):
    import concourse.bacc as bacc
    from concourse.bass_utils import run_bass_kernel_spmd

    a = {name.removeprefix("L0_attn_").removeprefix("L0_ffn_"): np.asarray(v) for name, v in inputs.items()}
    tokens = a["hidden"].reshape(T, D)
    head_of = np.array([[KVH * j + c for j in range(KVH)] for c in range(REP)]).reshape(-1)
    pair_first = np.concatenate([np.arange(0, HD, 2), np.arange(1, HD, 2)])
    q_cols = (head_of[:, None] * HD + pair_first[None, :]).reshape(-1)
    k_cols = (np.arange(KVH)[:, None] * HD + pair_first[None, :]).reshape(-1)
    wide_heads = np.array([[[KVH * j + 2 * cb + pl for pl in range(2)] for j in range(KVH)] for cb in range(2)]).reshape(-1)
    g_rows, l_rows = ((h[:, None] * HD + np.arange(HD)[None, :]).reshape(-1) for h in (wide_heads, head_of))
    con = constants()
    ins = {
        "x_tok": tokens,
        "x_feat": tokens.T,
        "w_qkv1": a["g_wq"][:, q_cols],
        "w_kv_down_t": a["g_kv_down"].T,
        "w_kv_up": np.concatenate([a["g_k_up"][:, k_cols], a["g_v_up"]], 1),
        "w_qkv2": np.concatenate([a["l_wq"][:, q_cols], a["l_wk"][:, k_cols], a["l_wv"]], 1),
        "wo": np.concatenate([a["g_wo"][g_rows], a["l_wo"][l_rows]], 1),
        "norm_w": np.stack([a["norm1_w"], a["norm2_w"]], 1),
        "router_t": a["router_w"].T,
        "gate_t": a["gate_w"].transpose(2, 0, 1).reshape(D, E * F),
        "up_t": a["up_w"].transpose(2, 0, 1).reshape(D, E * F),
        "down_t": a["down_w"].transpose(2, 0, 1).reshape(FC, P, E, D).transpose(1, 2, 0, 3).reshape(P, E * FC * D),
        **con,
    }
    nc = bacc.Bacc("TRN2", target_bir_lowering=False, num_devices=1)
    arrays, args = {}, {}
    for name, v in ins.items():
        arrays[f"in_{name}"] = np.ascontiguousarray(v)
        args[name] = nc.dram_tensor(f"in_{name}", v.shape, mybir.dt.from_np(v.dtype), kind="ExternalInput").ap()
    args["out"] = nc.dram_tensor("out_0", (B, S, D), F32, kind="ExternalOutput").ap()
    block_program(nc, **args)
    return run_bass_kernel_spmd(nc, [arrays], core_ids=[0]).results[0]["out_0"]
```

```python
from contextlib import ExitStack

import concourse.bass as bass
import numpy as np
from concourse import mybir

ALU = mybir.AluOpType
ACT = mybir.ActivationFunctionType
AX = mybir.AxisListType
F32 = mybir.dt.float32
F16 = mybir.dt.float16
I32 = mybir.dt.int32
U32 = mybir.dt.uint32

P = 128
D = 128
H, KVH, HD = 16, 4, 8
REP = H // KVH
LAT = 32
WIN = 32
B, S = 4, 512
T = B * S
QT = S // P
HALVES = 2
PASSES = B // HALVES
NH = H + KVH
E, F = 8, 512
FC = F // P
QKV = NH * HD + KVH * HD
TERMS = 4
HW = TERMS * HD
SCALE = float(np.float32(1.0) / np.sqrt(np.float32(HD)))
BASES = (1000000.0, 10000.0)
RMS_EPS, LN_EPS = 1e-6, 1e-5
MASKED = -30000.0
PAD = 64
BLK = 64
MB = S // BLK

ROW = 132
CAP = T + P
PADROW = E * CAP
TILES = (2 * T + E * (P - 1)) // P
assert TILES == 39

GROUPS = (24, MB)


def rope_tables():
    out = np.empty((P, 2, 2, QT, HD // 2), np.float32)
    for l, base in enumerate(BASES):
        inv = (np.float32(1.0) / np.power(np.float32(base), np.arange(0, HD, 2, dtype=np.float32) / np.float32(HD))).astype(np.float32)
        ang = (np.arange(S, dtype=np.float32)[:, None] * inv[None, :]).astype(np.float32)
        for n, f in enumerate((np.cos, np.sin)):
            out[:, l, n] = f(ang).astype(np.float32).reshape(QT, P, HD // 2).transpose(1, 0, 2)
    return out


def window_bias():
    key = np.arange(P)[:, None] - BLK
    diff = np.arange(BLK)[None, :] - key
    block = np.where((diff >= 0) & (diff < WIN), 0.0, MASKED).astype(np.float16)
    return np.ascontiguousarray(np.broadcast_to(block[:, None, :], (P, REP, BLK)).reshape(P, REP * BLK))


def constants():
    upper = np.triu(np.ones((P, P)), 1)
    shift = np.zeros((P, 4 * E), np.float32)
    shift[:, 0:E] = np.arange(E) * CAP
    shift[:, E:2 * E] = np.arange(E, 0, -1)
    shift[:, 2 * E] = T + np.arange(P)
    return {
        "rope": rope_tables(),
        "eye": np.eye(P, dtype=np.float32),
        "ones": np.ones((P, P), np.float32),
        "half": np.concatenate([np.eye(P), upper, np.ones((P, P))], 1).astype(np.float16),
        "window": window_bias(),
        "expert": shift,
        "tile_no": np.broadcast_to(np.arange(TILES, dtype=np.float32)[:, None], (P, TILES, E)).reshape(P, TILES * E).copy(),
        "ids": np.arange(T, dtype=np.float32).reshape(T // P, P).T.copy(),
    }


class Event:

    def __init__(self, sem, per, skip=0, start=0):
        self.sem, self.per, self.skip, self.start = sem, per, skip, start

    def at(self, it, k):
        return it * self.per + (self.start + self.skip + k)


class Chain:

    def __init__(self, eng, sem, it=0, per=0, base=0):
        self.eng, self.sem, self.it, self.per, self.n, self.base = eng, sem, it, per, 0, base

    def do(self, ins):
        ins.then_inc(self.sem, 1)
        self.n += 1

    def sync(self):
        self.eng.wait_ge(self.sem, self.it * self.per + (self.base + self.n))

    def step(self, ins):
        self.do(ins)
        self.sync()


def tell(eng, ins, event, it, k):
    ins.then_inc(event.sem, 1)
    eng.wait_ge(event.sem, event.at(it, k))


def load_tables(act, which):
    name = act.bass.get_next_instruction_name()
    act.add_instruction(mybir.InstLoadActFuncSet(act_func_set_id=which, name=name, engine=mybir.EngineType.Activation))


class Lease:

    def __init__(self, last, per_pass_last):
        self.event, self.k = last, per_pass_last
        self.before_pass = True

    def wait_free(self, pe, it):
        k = self.k - (self.event.per if self.before_pass else 0)
        assert self.event.skip + k >= 0
        pe.wait_ge(self.event.sem, self.event.at(it, k))

    def lend(self, event, k):
        self.event, self.k, self.before_pass = event, k, False


def block_program(nc: bass.Bass, x_tok, x_feat, w_qkv1, w_kv_down_t, w_kv_up, w_qkv2, wo, norm_w,
                  router_t, gate_t, up_t, down_t, rope, eye, ones, half, window, expert, tile_no, ids, out):
    rows = nc.dram_tensor("routed_rows", [E * CAP + P, ROW], F32, kind="Internal").ap()
    acc = nc.dram_tensor("residual_rows", [T + P, D], F32, kind="Internal").ap()

    with ExitStack() as ctx:
        def sb(name, shape, dt=F32):
            return ctx.enter_context(nc.sbuf_tensor(name, shape, dt))

        def sem(name):
            return ctx.enter_context(nc.semaphore(name))

        def events(name, per1, per2, start=0):
            sems = [sem(f"{name}{u}") for u in range(HALVES)]
            return [[Event(sems[u], per1 + per2, l * per1, start) for u in range(HALVES)] for l in range(2)]

        rope_sb = sb("rope_sb", [P, 2, 2, QT, HD // 2])
        eye_sb = sb("eye_sb", [P, P])
        ones_sb = sb("ones_sb", [P, P])
        half_sb = sb("half_sb", [P, 3, P], F16)
        window_sb = sb("window_sb", [P, REP * BLK], F16)
        expert_sb = sb("expert_sb", [P, 4 * E])
        tile_no_sb = sb("tile_no_sb", [P, TILES, E])
        ids_sb = sb("ids_sb", [P, T // P])
        wq1 = sb("wq1", [P, D])
        down_sb = sb("down_sb", [LAT, D])
        up_kv_sb = sb("up_kv_sb", [LAT, 2 * KVH * HD])
        wraw2 = sb("wraw2", [P, QKV])
        wqkv = sb("wqkv", [P, 2, QKV])
        wo_sb = sb("wo_sb", [P, 2, D])
        norm_sb = sb("norm_sb", [P, 2])
        router_sb = sb("router_sb", [P, E])
        gate_sb = sb("gate_sb", [P, E * F])
        up_sb = sb("up_sb", [P, E * F])
        mlp_down_sb = sb("mlp_down_sb", [P, E * FC * D])
        pad_rows = sb("pad_rows", [P, ROW])
        eye16, before16, ones16 = (half_sb[:, n, :] for n in range(3))

        x_in = [sb(f"x_in{u}", [P, QT, D]) for u in range(HALVES)]
        xT = [sb(f"xT{u}", [P, S]) for u in range(HALVES)]
        x2 = [sb(f"x2_{u}", [P, QT, D]) for u in range(HALVES)]
        x1 = [sb(f"x1_{u}", [P, QT, ROW]) for u in range(HALVES)]
        xsq = [sb(f"xsq{u}", [P, QT, D]) for u in range(HALVES)]
        raw = [sb(f"raw{u}", [P, QT, QKV]) for u in range(HALVES)]
        sq = [sb(f"sq{u}", [P, QT, NH * HD]) for u in range(HALVES)]
        ms = [sb(f"ms{u}", [P, QT, NH + 1]) for u in range(HALVES)]
        inv = [sb(f"inv{u}", [P, QT, NH + 1]) for u in range(HALVES)]
        t_a = sb("t_a", [P, QT * (NH + 1)])
        t_b = sb("t_b", [P, QT * (NH + 1)])
        qn = sb("qn", [P, QT, NH, HD])
        by_cos = sb("by_cos", [P, QT, NH, HD])
        by_sin = sb("by_sin", [P, QT, NH, HD])
        rot = sb("rot", [P, QT, NH, HD])
        qk16 = [sb(f"qk16_{u}", [P, QT, NH, TERMS, HD], F16) for u in range(HALVES)]
        qT = [sb(f"qT{u}", [P, REP, S], F16) for u in range(HALVES)]
        kT = [sb(f"kT{u}", [P, KVH, PAD + S], F16) for u in range(HALVES)]
        v1 = [sb(f"v1_{u}", [P, QT, KVH, 2, HW]) for u in range(HALVES)]
        v2 = [sb(f"v2_{u}", [P, MB, KVH, HW]) for u in range(HALVES)]
        PN = 6
        probs = [sb(f"probs{n}", [P, 1024]) for n in range(PN)]
        o_sb = [[sb(f"o_sb{l}_{n}", [P, S]) for n in range((2, QT)[l])] for l in range(2)]
        rden = sb("rden", [P, QT * H])
        on = sb("on", [P, QT, D])
        oT = sb("oT", [P, S])
        z = sb("z", [P, QT, D])
        zc = sb("zc", [P, QT, D])
        ln_s = sb("ln_s", [P, 4, QT])
        x1T = sb("x1T", [P, S])
        lg = sb("lg", [P, QT, E])
        r_t = [sb(f"r_t{n}", [P, QT, E]) for n in range(4)]
        sel = [sb(f"sel{n}", [P, QT, E]) for n in range(2)]
        sel16 = sb("sel16", [P, QT, E], F16)
        r_s = sb("r_s", [P, 8, QT])
        run = sb("run", [P, QT + 1, E])
        wacc = sb("wacc", [P, QT, E])
        slot = [sb(f"slot{u}", [P, 2, QT], U32) for u in range(HALVES)]

        ps_s = ctx.enter_context(nc.psum_tensor("ps_s", [P, 2, 1024], F32))
        ps_o = ctx.enter_context(nc.psum_tensor("ps_o", [P, 2, 512], F32))
        ps_w = ctx.enter_context(nc.psum_tensor("ps_w", [P, 2, 512], F32))

        loaded = {n: sem(f"loaded_{n}") for n in ("consts", "attn", "mlp")}
        weights_ready = sem("weights_ready")
        fold_ready = sem("fold_ready")
        pad_set = sem("pad_set")
        x_loaded = [Event(sem(f"x_loaded{u}"), 32) for u in range(HALVES)]
        qkv_ready = events("qkv_ready", 2, 2)
        raw_ready = events("raw_ready", 2, 2)
        sq_ready = events("sq_ready", 2, 2)
        arg_ready = events("arg_ready", 1, 1, start=1)
        ln_ready = events("ln_ready", 1, 1)
        guess_ready = events("guess_ready", 1, 1)
        inv_ready = events("inv_ready", 1, 1)
        v_ready = events("v_ready", 1, 1, start=1)
        split_ready = events("split_ready", 1, 1, start=1)
        turned = events("turned", 3, 3)
        qT_a = events("qT_a", 1, 1)
        qT_b = events("qT_b", 1, 1)
        kT_ready = events("kT_ready", 1, 1)
        scores = Event(sem("scores"), 2 * sum(GROUPS))
        exped = Event(sem("exped"), 2 * sum(GROUPS), start=1)
        masked = [Event(sem(f"masked{u}"), GROUPS[0]) for u in range(HALVES)]
        pv = Event(sem("pv"), 2 * sum(GROUPS), start=1)
        o_out = [[Event(sem(f"o_out{l}_{u}"), (2, QT)[l], start=l) for u in range(HALVES)] for l in range(2)]
        o_turned = [[Event(sem(f"o_turned{l}_{u}"), (2, QT)[l], start=l) for u in range(HALVES)] for l in range(2)]
        on_part = events("on_part", 2, 4)
        on_turned = events("on_turned", 1, 1)
        oT_ready = events("oT_ready", 1, 1)
        proj_ready = events("proj_ready", 1, 1)
        x2_ready = [Event(sem(f"x2_ready{u}"), 1) for u in range(HALVES)]
        x2_turned = [Event(sem(f"x2_turned{u}"), 1) for u in range(HALVES)]
        x2T_ready = [Event(sem(f"x2T_ready{u}"), 1) for u in range(HALVES)]
        z_ready = [Event(sem(f"z_ready{u}"), 1) for u in range(HALVES)]
        zc_ready = [Event(sem(f"zc_ready{u}"), 1) for u in range(HALVES)]
        zsq_ready = [Event(sem(f"zsq_ready{u}"), 1) for u in range(HALVES)]
        zarg_ready = [Event(sem(f"zarg_ready{u}"), 1) for u in range(HALVES)]
        zln_ready = [Event(sem(f"zln_ready{u}"), 1) for u in range(HALVES)]
        zguess_ready = [Event(sem(f"zguess_ready{u}"), 1) for u in range(HALVES)]
        x1_ready = [Event(sem(f"x1_ready{u}"), 1, start=1) for u in range(HALVES)]
        x1_turned = [Event(sem(f"x1_turned{u}"), 1) for u in range(HALVES)]
        x1T_ready = [Event(sem(f"x1T_ready{u}"), 1) for u in range(HALVES)]
        logits_ready = [Event(sem(f"logits_ready{u}"), 1) for u in range(HALVES)]
        logits_out = [Event(sem(f"logits_out{u}"), 1, start=1) for u in range(HALVES)]
        gap_ready = [Event(sem(f"gap_ready{u}"), 1) for u in range(HALVES)]
        ratio_ready = [Event(sem(f"ratio_ready{u}"), 1) for u in range(HALVES)]
        sel_ready = [Event(sem(f"sel_ready{u}"), 1) for u in range(HALVES)]
        ranks_ready = [Event(sem(f"ranks_ready{u}"), 1) for u in range(HALVES)]
        ranks_out = [Event(sem(f"ranks_out{u}"), 1, start=1) for u in range(HALVES)]
        slots_ready = [Event(sem(f"slots_ready{u}"), 1) for u in range(HALVES)]
        scattered = [Event(sem(f"scattered{u}"), 2 * QT * 16) for u in range(HALVES)]
        stored = [Event(sem(f"stored{u}"), 16) for u in range(HALVES)]
        x1_free = [Event(sem(f"x1_free{u}"), 2, start=2) for u in range(HALVES)]
        dve_own = sem("dve_own")
        act_own = sem("act_own")
        pool_own = sem("pool_own")
        pool_passed = sem("pool_passed")

        first = {(0, 0): 0, (0, 1): GROUPS[0], (1, 0): 2 * GROUPS[0], (1, 1): 2 * GROUPS[0] + GROUPS[1]}
        LAG = 3

        te_sb = sb("te_sb", [P, TILES + 1], I32)
        row_sb = sb("row_sb", [P, TILES + 1], I32)
        end_sb = sb("end_sb", [P, E], I32)
        mean_w = sb("mean_w", [P, E])
        c_f = [sb(f"c_f{n}", [P, E]) for n in range(4)]
        c_i = sb("c_i", [P, E], I32)
        c_t = [sb(f"c_t{n}", [P, TILES, E]) for n in range(3)]
        c_r = [sb(f"c_r{n}", [P, TILES + 1]) for n in range(2)]
        xs = [sb(f"xs{n}", [P, ROW]) for n in range(2)]
        xsT = [sb(f"xsT{n}", [P, P]) for n in range(2)]
        idu = [sb(f"idu{n}", [P, 1], U32) for n in range(2)]
        tile_ids = sb("tile_ids", [P, TILES + 1])
        ys = [sb(f"ys{n}", [P, D]) for n in range(2)]
        sg = [probs[n][:, 0:F] for n in range(2)]
        hid = [probs[2 + n][:, 0:F] for n in range(2)]
        hT = [probs[4 + n][:, 0:F] for n in range(2)]
        counted = sem("counted")
        wsum_ready = sem("wsum_ready")
        tables = sem("tables")
        padded = sem("padded")
        xs_loaded = [sem(f"xs_loaded{n}") for n in range(2)]
        xs_turned = sem("xs_turned")
        xsT_ready = sem("xsT_ready")
        ids_kept = sem("ids_kept")
        idu_ready = sem("idu_ready")
        gate_ready = sem("gate_ready")
        up_ready = sem("up_ready")
        silu_ready = sem("silu_ready")
        hid_ready = sem("hid_ready")
        hid_turned = sem("hid_turned")
        hT_ready = sem("hT_ready")
        y_ready = sem("y_ready")
        ys_ready = sem("ys_ready")
        added = sem("added")
        dump_set = sem("dump_set")
        fin_loaded = [sem(f"fin_loaded{u}") for u in range(B)]
        fin_c = sem("fin_c")
        fin_sq = sem("fin_sq")
        fin_arg = sem("fin_arg")
        fin_guess = sem("fin_guess")
        fin_ready = sem("fin_ready")
        fin_stored = sem("fin_stored")
        fin_z = [(x_in[0], x2[0]), (x_in[1], x2[1]), (z, zc), (xsq[0], xsq[1])]

        def groups1(n):
            c, g = divmod(n, 6)
            kt, js = [(0, (0, 1)), (0, (2, 3)), (1, (0, 1)), (1, (2, 3)), (2, (0, 1, 2, 3)), (3, (0, 1, 2, 3))][g]
            width = S - P * kt
            return kt, c, js, width, (512 if len(js) == 2 else width)

        def prob_heads(g, count, step, width):
            return probs[g % PN][:, 0:count * step].rearrange("p (h n) -> p h n", n=step)[:, :, 0:width]

        block = ctx.enter_context(nc.Block())

        @block.sync
        def _(sp):
            for dst, src in ((wq1[:, :], w_qkv1), (down_sb[:, :], w_kv_down_t), (up_kv_sb[:, :], w_kv_up),
                             (norm_sb[:, :], norm_w), (rope_sb[:, :, :, :, :], rope), (eye_sb[:, :], eye),
                             (half_sb[:, :, :], half.rearrange("p (n m) -> p n m", n=3)), (wraw2[:, :], w_qkv2),
                             (expert_sb[:, :], expert), (ids_sb[:, :], ids)):
                sp.dma_start(dst, src).then_inc(loaded["consts"], 16)
            for u in range(HALVES):
                sp.sem_inc(x1_free[u].sem, 1)
            with sp.Fori(0, PASSES) as it:
                for u in range(HALVES):
                    sp.wait_ge(x1_ready[u].sem, x1_ready[u].at(it, 0))
                    tok = (it * HALVES + u) * S
                    sp.dma_start(x_in[u][:, :, :], x_tok[bass.ds(tok, S), :].rearrange("(t p) d -> p t d", p=P)).then_inc(x_loaded[u].sem, 16)
                    sp.dma_start(xT[u][:, :], x_feat[:, bass.ds(tok, S)]).then_inc(x_loaded[u].sem, 16)
                for u in range(HALVES):
                    sp.wait_ge(x1_ready[u].sem, x1_ready[u].at(it, 1))
                    tok = (it * HALVES + u) * S
                    sp.dma_start(acc[bass.ds(tok, S), :].rearrange("(t p) d -> p t d", p=P), x1[u][:, :, 0:D]).then_inc(stored[u].sem, 16)
                for u in range(HALVES):
                    sp.wait_ge(stored[u].sem, stored[u].at(it, 16))
                    sp.sem_inc(x1_free[u].sem, 1)
            sp.wait_ge(pad_set, 1)
            sp.dma_start(rows[PADROW:PADROW + P, :], pad_rows[:, :]).then_inc(padded, 16)
            sp.dma_start(acc[T:T + P, :], pad_rows[:, 0:D]).then_inc(dump_set, 16)
            sp.wait_ge(tables, 1)
            for e in range(E):
                end = sp.value_load(end_sb[0:1, e:e + 1], min_val=e * CAP, max_val=e * CAP + T)
                sp.dma_start(rows[bass.ds(end, P), :], pad_rows[:, :]).then_inc(padded, 16)
            for u in range(HALVES):
                sp.wait_ge(scattered[u].sem, scattered[u].per * PASSES)
            sp.wait_ge(tables, 2)
            sp.wait_ge(padded, 16 * (E + 1))

            def load_tile(i, n):
                row = sp.value_load(row_sb[0:1, bass.ds(i, 1)], min_val=0, max_val=PADROW)
                sp.dma_start(xs[n][:, :], rows[bass.ds(row, P), :]).then_inc(xs_loaded[n], 16)

            load_tile(0, 0)
            load_tile(1, 1)
            with sp.Fori(0, (TILES - 1) // 2) as k:
                for n in range(2):
                    sp.wait_ge(xs_turned, 2 * k + (n + 1))
                    sp.wait_ge(ids_kept, 2 * k + (n + 1))
                    load_tile(2 * k + (n + 2), n)
            sp.wait_ge(added, 16 * TILES)
            for b in range(B):
                sp.dma_start(fin_z[b][0][:, :, :], acc[b * S:(b + 1) * S, :].rearrange("(t p) d -> p t d", p=P)).then_inc(fin_loaded[b], 16)
            for b in range(B):
                sp.wait_ge(fin_ready, b + 1)
                sp.dma_start(out[b, :, :].rearrange("(t p) d -> p t d", p=P), fin_z[b][0][:, :, :]).then_inc(fin_stored, 16)
            sp.wait_ge(fin_stored, 16 * B)
            for u in range(HALVES):
                sp.wait_ge(stored[u].sem, stored[u].per * PASSES)

        @block.gpsimd
        def _(pool):
            for u in range(HALVES):
                nc.gpsimd.memset(kT[u][:, :, :].bitcast(F32), 0.0).then_inc(pool_own, 1)
                nc.gpsimd.memset(v2[u][:, :, :, :], 0.0).then_inc(pool_own, 1)
                nc.gpsimd.memset(v1[u][:, :, :, :, :], 0.0).then_inc(pool_own, 1)
            pool.wait_ge(pool_own, 6)
            for u in range(HALVES):
                nc.gpsimd.memset(v1[u][:, :, :, 0, HD:HD + 1], 1.0).then_inc(pool_own, 1)
                nc.gpsimd.memset(v1[u][:, :, :, 1, 3 * HD:3 * HD + 1], 1.0).then_inc(pool_own, 1)
                nc.gpsimd.memset(v2[u][:, 1:MB, :, HD:HD + 1], 1.0).then_inc(pool_own, 1)
            pool.wait_ge(pool_own, 12)
            for u in range(HALVES):
                nc.gpsimd.memset(v2[u][BLK:P, 0:1, :, HD:HD + 1], 1.0).then_inc(pool_own, 1)
            pool.wait_ge(pool_own, 14)
            pool.wait_ge(weights_ready, 3)
            pool.wait_ge(loaded["attn"], 16 * ATTN_LOADS)
            pool.dma_start(gate_sb[:, :], gate_t).then_inc(loaded["mlp"], 16)
            pool.dma_start(up_sb[:, :], up_t).then_inc(loaded["mlp"], 16)
            pool.dma_start(mlp_down_sb[:, :], down_t).then_inc(loaded["mlp"], 16)

            def masks(it, u):
                for n in range(GROUPS[0]):
                    kt, c, js, width, step = groups1(n)
                    g = first[0, u] + n
                    pool.wait_ge(exped.sem, exped.at(it, g + 1))
                    pool.sem_inc(pool_passed, 1)
                    tri = prob_heads(g, len(js), step, P)
                    nc.gpsimd.affine_select(out=tri, in_=tri, compare_op=ALU.is_ge, fill=0.0, base=0,
                                            pattern=[[0, len(js)], [1, P]], channel_multiplier=-1).then_inc(masked[u].sem, 1)

            def scatter(it, u):
                pool.wait_ge(slots_ready[u].sem, slots_ready[u].at(it, 1))
                pool.sem_inc(pool_passed, 1)
                for t in range(QT):
                    for k in range(2):
                        nc.gpsimd.indirect_dma_start(rows, bass.IndirectOffsetOnAxis(ap=slot[u][:, k, t:t + 1], axis=0),
                                                     x1[u][:, t, :], None).then_inc(scattered[u].sem, 16)

            for u in range(HALVES):
                pool.sem_inc(x1_free[u].sem, 1)
            with pool.Fori(0, PASSES) as it:
                masks(it, 0)
                masks(it, 1)
                scatter(it, 0)
                scatter(it, 1)
                for u in range(HALVES):
                    pool.wait_ge(scattered[u].sem, scattered[u].at(it, scattered[u].per))
                    pool.sem_inc(x1_free[u].sem, 1)

            for u in range(HALVES):
                pool.wait_ge(stored[u].sem, stored[u].per * PASSES)

            def add_tile(i, n, first=False):
                pool.wait_ge(idu_ready, i + 1)
                pool.wait_ge(ys_ready, i + 1)
                if not first:
                    pool.wait_ge(added, 16 * i)
                pool.sem_inc(pool_passed, 1)
                nc.gpsimd.indirect_dma_start(acc, bass.IndirectOffsetOnAxis(ap=idu[n][:, 0:1], axis=0), ys[n][:, :], None,
                                             compute_op=ALU.add).then_inc(added, 16)

            pool.wait_ge(dump_set, 16)
            add_tile(0, 0, first=True)
            with pool.Fori(0, (TILES - 1) // 2) as k:
                for n in (1, 2):
                    add_tile(2 * k + n, n % 2)

        @block.tensor
        def _(pe):
            pe.wait_ge(loaded["consts"], 16 * CONSTS)
            nc.tensor.matmul(ps_w[:, 0, 0:2 * KVH * HD], down_sb[:, :], up_kv_sb[:, :], start=True, stop=True).then_inc(fold_ready, 1)

            w = [Lease(ranks_out[1], 1), Lease(logits_out[1], 1)]
            o = [Lease(o_out[1][1], 4), Lease(o_out[1][1], 4)]

            def turn_x2(it, u):
                pe.wait_ge(x2_ready[u].sem, x2_ready[u].at(it, 1))
                w[0].wait_free(pe, it)
                for t in range(QT):
                    last = nc.tensor.transpose(ps_w[:, 0, P * t:P * t + P], x2[u][:, t, :], eye_sb[:, :])
                last.then_inc(x2_turned[u].sem, 1)
                w[0].lend(x2T_ready[u], 1)

            def project(it, l, u):
                if l == 0:
                    pe.wait_ge(x_loaded[u].sem, x_loaded[u].at(it, 32))
                else:
                    pe.wait_ge(x2T_ready[u].sem, x2T_ready[u].at(it, 1))
                for n in range(2):
                    w[n].wait_free(pe, it)
                    for t in range(2):
                        tile = 2 * n + t
                        last = nc.tensor.matmul(ps_w[:, n, 256 * t:256 * t + QKV], xT[u][:, P * tile:P * tile + P],
                                                wqkv[:, l, :], start=True, stop=True)
                    last.then_inc(qkv_ready[l][u].sem, 1)
                    w[n].lend(raw_ready[l][u], n + 1)

            def turn_queries(it, l, u):
                pe.wait_ge(split_ready[l][u].sem, split_ready[l][u].at(it, 1))
                flat = qk16[u][:, :, :, :, :].rearrange("p t h m d -> p t (h m d)")
                for n in range(2):
                    w[n].wait_free(pe, it)
                    bank = ps_w[:, n, :].bitcast(F16)
                    for t in range(2):
                        for c in range(REP):
                            last = nc.tensor.transpose(bank[:, 256 * c + P * t:256 * c + P * t + P],
                                                       flat[:, 2 * n + t, P * c:P * c + P], eye16)
                    last.then_inc(turned[l][u].sem, 1)
                    w[n].lend((qT_a, qT_b)[n][l][u], 1)

            def turn_keys(it, l, u):
                flat = qk16[u][:, :, :, :, :].rearrange("p t h m d -> p t (h m d)")
                w[0].wait_free(pe, it)
                bank = ps_w[:, 0, :].bitcast(F16)
                for t in range(QT):
                    last = nc.tensor.transpose(bank[:, P * t:P * t + P], flat[:, t, REP * P:REP * P + P], eye16)
                last.then_inc(turned[l][u].sem, 1)
                w[0].lend(kT_ready[l][u], 1)

            def attend(it, l, u, beside):
                pe.wait_ge(loaded["attn"], 16 * ATTN_LOADS)
                for event in (qT_a, qT_b, kT_ready):
                    pe.wait_ge(event[l][u].sem, event[l][u].at(it, 1))

                def score(n):
                    g = first[l, u] + n
                    pe.wait_ge(exped.sem, exped.at(it, max(g - 1, 0)))
                    if l == 0:
                        kt, c, js, width, step = groups1(n)
                        for h, j in enumerate(js):
                            last = nc.tensor.matmul(ps_s[:, g % 2, step * h:step * h + width],
                                                    kT[u][:, j, PAD + P * kt:PAD + P * kt + P],
                                                    qT[u][:, c, P * kt:S], start=True, stop=True)
                    else:
                        for j in range(KVH):
                            nc.tensor.matmul(ps_s[:, g % 2, 256 * j:256 * j + 256], eye16, window_sb[:, 0:REP * BLK],
                                             start=True, stop=False)
                            last = nc.tensor.matmul(ps_s[:, g % 2, 256 * j:256 * j + 256],
                                                    kT[u][:, j, BLK * n:BLK * n + P],
                                                    qT[u][:, :, BLK * n:BLK * n + BLK], start=False, stop=True)
                    last.then_inc(scores.sem, 1)

                def value(n):
                    g = first[l, u] + n
                    p = probs[g % PN]
                    if l == 0:
                        pe.wait_ge(masked[u].sem, masked[u].at(it, n + 1))
                        kt, c, js, width, step = groups1(n)
                        if n % 12 == 0:
                            o[c // 2].wait_free(pe, it)
                        for h, j in enumerate(js):
                            last = nc.tensor.matmul(ps_o[32 * j:32 * j + HW, c // 2, P * kt:S], v1[u][:, kt, j, c % 2, :],
                                                    p[:, step * h:step * h + width],
                                                    start=(kt == 0 and c % 2 == 0), stop=(kt == QT - 1 and c % 2 == 1),
                                                    skip_group_check=True)
                        if n % 12 == 11:
                            o[c // 2].lend(o_out[0][u], c // 2 + 1)
                    else:
                        pe.wait_ge(exped.sem, exped.at(it, g + 1))
                        t = n // 2
                        if n % 2 == 0:
                            o[t % 2].wait_free(pe, it)
                        for j in range(KVH):
                            last = nc.tensor.matmul(ps_o[32 * j:32 * j + HW, t % 2, 256 * (n % 2):256 * (n % 2) + 256],
                                                    v2[u][:, n, j, :], p[:, 256 * j:256 * j + 256], start=True, stop=True,
                                                    skip_group_check=True)
                        if n % 2 == 1:
                            o[t % 2].lend(o_out[1][u], t + 1)
                    last.then_inc(pv.sem, 1)

                count = GROUPS[l]
                for n in range(count + LAG):
                    if n < count:
                        score(n)
                    if n == LAG:
                        pe.wait_ge(v_ready[l][u].sem, v_ready[l][u].at(it, 1))
                    if n >= LAG:
                        value(n - LAG)
                    beside(n)

            def turn_outputs(it, l, u, ns):
                for n in ns:
                    pe.wait_ge(o_out[l][u].sem, o_out[l][u].at(it, (2, n + 1)[l]))
                    w[n % 2].wait_free(pe, it)
                    for k in range(4):
                        if l == 0:
                            src = o_sb[0][k % 2][:, P * (2 * n + k // 2):P * (2 * n + k // 2) + P]
                        else:
                            src = o_sb[1][n][:, P * k:P * k + P]
                        last = nc.tensor.transpose(ps_w[:, n % 2, P * k:P * k + P], src, eye_sb[:, :])
                    last.then_inc(o_turned[l][u].sem, 1)
                    w[n % 2].lend(on_part[l][u], n + 1)

            def turn_normalised(it, l, u):
                pe.wait_ge(on_part[l][u].sem, on_part[l][u].at(it, (2, 4)[l]))
                w[0].wait_free(pe, it)
                for t in range(QT):
                    last = nc.tensor.transpose(ps_w[:, 0, P * t:P * t + P], on[:, t, :], eye_sb[:, :])
                last.then_inc(on_turned[l][u].sem, 1)
                w[0].lend(oT_ready[l][u], 1)

            def project_outputs(it, l, u):
                pe.wait_ge(oT_ready[l][u].sem, oT_ready[l][u].at(it, 1))
                w[1].wait_free(pe, it)
                for t in range(QT):
                    last = nc.tensor.matmul(ps_w[:, 1, P * t:P * t + P], oT[:, P * t:P * t + P], wo_sb[:, l, :], start=True, stop=True)
                last.then_inc(proj_ready[l][u].sem, 1)
                w[1].lend((x2_ready, z_ready)[l][u], 1)

            def turn_x1(it, u):
                pe.wait_ge(x1_ready[u].sem, x1_ready[u].at(it, 1))
                w[0].wait_free(pe, it)
                for t in range(QT):
                    last = nc.tensor.transpose(ps_w[:, 0, P * t:P * t + P], x1[u][:, t, 0:D], eye_sb[:, :])
                last.then_inc(x1_turned[u].sem, 1)
                w[0].lend(x1T_ready[u], 1)

            def router_logits(it, u):
                pe.wait_ge(x1T_ready[u].sem, x1T_ready[u].at(it, 1))
                w[1].wait_free(pe, it)
                for t in range(QT):
                    last = nc.tensor.matmul(ps_w[:, 1, E * t:E * t + E], x1T[:, P * t:P * t + P], router_sb[:, :], start=True, stop=True)
                last.then_inc(logits_ready[u].sem, 1)
                w[1].lend(logits_out[u], 1)

            def ranks(it, u):
                pe.wait_ge(sel_ready[u].sem, sel_ready[u].at(it, 1))
                w[0].wait_free(pe, it)
                chosen = sel16[:, :, :].rearrange("p t e -> p (t e)")
                nc.tensor.matmul(ps_w[:, 0, 0:QT * E], before16, chosen, start=True, stop=True)
                nc.tensor.matmul(ps_w[:, 0, 64:64 + QT * E], ones16, chosen, start=True, stop=True).then_inc(ranks_ready[u].sem, 1)
                w[0].lend(ranks_out[u], 1)

            pe.wait_ge(weights_ready, 3)
            pe.sem_inc(pv.sem, 1)
            for u in range(HALVES):
                pe.sem_inc(o_turned[1][u].sem, 1)
            with pe.Fori(0, PASSES) as it:
                project(it, 0, 0)
                turn_queries(it, 0, 0)
                turn_keys(it, 0, 0)

                def prepare_next(n):
                    if n == 0:
                        project(it, 0, 1)
                    if n == 18:
                        turn_queries(it, 0, 1)
                    if n == 19:
                        turn_keys(it, 0, 1)

                attend(it, 0, 0, prepare_next)

                def second_layer(u, steps):
                    def at_step(n):
                        if n == steps[0]:
                            turn_outputs(it, 0, u, (0, 1))
                        if n == steps[1]:
                            turn_normalised(it, 0, u)
                        if n == steps[2]:
                            project_outputs(it, 0, u)
                        if n == steps[3]:
                            turn_x2(it, u)
                        if n == steps[4]:
                            project(it, 1, u)
                        if n == steps[6]:
                            turn_queries(it, 1, u)
                        if n == steps[7]:
                            turn_keys(it, 1, u)
                    return at_step

                attend(it, 0, 1, second_layer(0, BESIDE_01))
                attend(it, 1, 0, second_layer(1, BESIDE_10))

                def finish_half(u, steps):
                    def at_step(n):
                        if n == steps[0]:
                            turn_outputs(it, 1, u, (0, 1))
                        if n == steps[1]:
                            turn_outputs(it, 1, u, (2, 3))
                        if n == steps[2]:
                            turn_normalised(it, 1, u)
                        if n == steps[3]:
                            project_outputs(it, 1, u)
                        if n == steps[6]:
                            turn_x1(it, u)
                        if n == steps[7]:
                            router_logits(it, u)
                        if n == steps[8]:
                            ranks(it, u)
                    return at_step

                attend(it, 1, 1, finish_half(0, BESIDE_11))
                last_half = finish_half(1, AFTER)
                for n in range(len(AFTER)):
                    last_half(n)

            pe.wait_ge(wsum_ready, 1)
            nc.tensor.matmul(ps_w[:, 1, 0:E], ones_sb[:, :], c_f[3][:, :], start=True, stop=True).then_inc(counted, 1)

            def turn_rows(i, n, pair):
                pe.wait_ge(xs_loaded[n], 16 * (pair + 1))
                pe.wait_ge(xsT_ready, i)
                nc.tensor.transpose(ps_w[:, 0, 0:P], xs[n][:, 0:D], eye_sb[:, :]).then_inc(xs_turned, 1)

            def gate_up(i, n):
                e = pe.value_load(te_sb[0:1, bass.ds(i, 1)], min_val=0, max_val=E - 1)
                pe.wait_ge(xsT_ready, i + 1)
                nc.tensor.matmul(ps_s[:, n, 0:F], xsT[n][:, :], gate_sb[:, bass.ds(e * F, F)], start=True, stop=True).then_inc(gate_ready, 1)
                nc.tensor.matmul(ps_s[:, n, F:2 * F], xsT[n][:, :], up_sb[:, bass.ds(e * F, F)], start=True, stop=True).then_inc(up_ready, 1)

            def turn_hidden(i, n):
                pe.wait_ge(hid_ready, i + 1)
                for f in range(FC):
                    last = nc.tensor.transpose(ps_o[:, n, P * f:P * f + P], hid[n][:, P * f:P * f + P], eye_sb[:, :])
                last.then_inc(hid_turned, 1)

            def down(i, n, first=False):
                e = pe.value_load(te_sb[0:1, bass.ds(i, 1)], min_val=0, max_val=E - 1)
                pe.wait_ge(hT_ready, i + 1)
                if not first:
                    pe.wait_ge(ys_ready, i)
                for f in range(FC):
                    last = nc.tensor.matmul(ps_w[:, 1, 0:D], hT[n][:, P * f:P * f + P],
                                            mlp_down_sb[:, bass.ds(e * (FC * D) + f * D, D)], start=(f == 0), stop=(f == FC - 1))
                last.then_inc(y_ready, 1)

            pe.wait_ge(tables, 3)
            pe.wait_ge(loaded["mlp"], 48)
            pe.wait_ge(xs_loaded[0], 16)
            nc.tensor.transpose(ps_w[:, 0, 0:P], xs[0][:, 0:D], eye_sb[:, :]).then_inc(xs_turned, 1)
            gate_up(0, 0)
            turn_rows(1, 1, 0)

            def tile_pair(k, first=False):
                for n in range(2):
                    turn_rows(2 * k + (n + 2), n, k + 1)
                    turn_hidden(2 * k + n, n)
                    gate_up(2 * k + (n + 1), 1 - n)
                    down(2 * k + n, n, first and n == 0)

            tile_pair(0, first=True)
            with pe.Fori(1, (TILES - 1) // 2) as k:
                tile_pair(k)
            turn_hidden(TILES - 1, 0)
            down(TILES - 1, 0)

        @block.scalar
        def _(act):
            for dst, src in ((wo_sb[:, :, :], wo.rearrange("p (l n) -> p l n", l=2)), (window_sb[:, :], window),
                             (router_sb[:, :], router_t),
                             (ones_sb[:, :], ones), (tile_no_sb[:, :, :], tile_no.rearrange("p (t e) -> p t e", e=E))):
                act.dma_start(dst, src).then_inc(loaded["attn"], 16)
            load_tables(act, LN_EXP_SET)

            def squares(it, l, u):
                if l == 0:
                    act.wait_ge(x_loaded[u].sem, x_loaded[u].at(it, 32))
                    act.wait_ge(arg_ready[0][u].sem, arg_ready[0][u].at(it, 0))
                    src = x_in[u]
                else:
                    act.wait_ge(x2_ready[u].sem, x2_ready[u].at(it, 1))
                    src = x2[u]
                nc.scalar.activation(xsq[u][:, :, :], src[:, :, :], ACT.Square).then_inc(sq_ready[l][u].sem, 1)

            def copy_x2(it, u):
                act.wait_ge(x2_turned[u].sem, x2_turned[u].at(it, 1))
                nc.scalar.copy(xT[u][:, :], ps_w[:, 0, :]).then_inc(x2T_ready[u].sem, 1)

            def copy_raw(it, l, u):
                act.wait_ge(split_ready[l][u].sem, split_ready[l][u].at(it, 0))
                act.wait_ge(v_ready[l][u].sem, v_ready[l][u].at(it, 0))
                for n in range(2):
                    act.wait_ge(qkv_ready[l][u].sem, qkv_ready[l][u].at(it, n + 1))
                    src = ps_w[:, n, :].rearrange("p (t n) -> p t n", t=2)[:, :, 0:QKV]
                    nc.scalar.copy(raw[u][:, 2 * n:2 * n + 2, :], src).then_inc(raw_ready[l][u].sem, 1)
                act.wait_ge(raw_ready[l][u].sem, raw_ready[l][u].at(it, 2))
                nc.scalar.activation(sq[u][:, :, :], raw[u][:, :, 0:NH * HD], ACT.Square).then_inc(sq_ready[l][u].sem, 1)

            def guess_root(it, l, u):
                act.wait_ge(arg_ready[l][u].sem, arg_ready[l][u].at(it, 1))
                nc.scalar.activation(inv[u][:, :, :], ms[u][:, :, :], ACT.Ln).then_inc(ln_ready[l][u].sem, 1)
                act.wait_ge(ln_ready[l][u].sem, ln_ready[l][u].at(it, 1))
                nc.scalar.activation(inv[u][:, :, :], inv[u][:, :, :], ACT.Exp, scale=-0.5).then_inc(guess_ready[l][u].sem, 1)

            def copy_queries(it, l, u):
                act.wait_ge(turned[l][u].sem, turned[l][u].at(it, 2))
                src = ps_w[:, 1, :].bitcast(F16).rearrange("p (c n) -> p c n", c=REP)
                nc.scalar.copy(qT[u][:, :, 256:512], src).then_inc(qT_b[l][u].sem, 1)

            def copy_outputs_of(it, u, t):
                act.wait_ge(pv.sem, pv.at(it, first[1, u] + 2 * (t + 1)))
                if t == 0:
                    act.wait_ge(o_turned[1][1 - u].sem, o_turned[1][1 - u].at(it, QT * u))
                src = ps_o[:, t % 2, :].rearrange("p (m c q) -> p m c q", m=2, c=REP)
                dst = o_sb[1][t][:, :].rearrange("p (c m q) -> p m c q", m=2, c=REP)
                nc.scalar.copy(dst, src).then_inc(o_out[1][u].sem, 1)

            def exponentials(it, l, u, beside):
                for n in range(GROUPS[l] + LAG):
                    if n < GROUPS[l]:
                        exponential(it, l, u, n)
                    t, odd = divmod(n - LAG, 2)
                    if l == 1 and t >= 0 and odd:
                        copy_outputs_of(it, u, t)
                    beside(n)

            def exponential(it, l, u, n):
                g = first[l, u] + n
                act.wait_ge(scores.sem, scores.at(it, g + 1))
                act.wait_ge(pv.sem, pv.at(it, max(g - PN + 1, 0)))
                if l == 0:
                    kt, c, js, width, step = groups1(n)
                else:
                    js, width, step = range(2), 512, 512
                src = ps_s[:, g % 2, 0:len(js) * step].rearrange("p (h n) -> p h n", n=step)[:, :, 0:width]
                nc.scalar.activation(prob_heads(g, len(js), step, width), src, ACT.Exp, scale=SCALE).then_inc(exped.sem, 1)

            def copy_outputs(it, l, u):
                act.wait_ge(on_turned[l][u].sem, on_turned[l][u].at(it, 1))
                nc.scalar.copy(oT[:, :], ps_w[:, 0, :]).then_inc(oT_ready[l][u].sem, 1)

            def square_z(it, u):
                act.wait_ge(zc_ready[u].sem, zc_ready[u].at(it, 1))
                nc.scalar.activation(z[:, :, :], zc[:, :, :], ACT.Square).then_inc(zsq_ready[u].sem, 1)

            def guess_norm(it, u):
                act.wait_ge(zarg_ready[u].sem, zarg_ready[u].at(it, 1))
                nc.scalar.activation(ln_s[:, 3, :], ln_s[:, 2, :], ACT.Ln).then_inc(zln_ready[u].sem, 1)
                act.wait_ge(zln_ready[u].sem, zln_ready[u].at(it, 1))
                nc.scalar.activation(ln_s[:, 3, :], ln_s[:, 3, :], ACT.Exp, scale=-0.5).then_inc(zguess_ready[u].sem, 1)

            def copy_x1(it, u):
                act.wait_ge(x1_turned[u].sem, x1_turned[u].at(it, 1))
                nc.scalar.copy(x1T[:, :], ps_w[:, 0, :]).then_inc(x1T_ready[u].sem, 1)

            def weight_ratio(it, u):
                act.wait_ge(gap_ready[u].sem, gap_ready[u].at(it, 1))
                nc.scalar.activation(r_s[:, 5, :], r_s[:, 4, :], ACT.Exp).then_inc(ratio_ready[u].sem, 1)

            act.sem_inc(exped.sem, 1)
            for u in range(HALVES):
                act.sem_inc(o_out[1][u].sem, 1)
            with act.Fori(0, PASSES) as it:
                squares(it, 0, 0)
                copy_raw(it, 0, 0)
                guess_root(it, 0, 0)
                copy_queries(it, 0, 0)

                def prepare_next(n):
                    if n == 0:
                        squares(it, 0, 1)
                        copy_raw(it, 0, 1)
                    if n == 4:
                        guess_root(it, 0, 1)
                    if n == 18:
                        copy_queries(it, 0, 1)

                exponentials(it, 0, 0, prepare_next)

                def second_layer(u, steps):
                    def at_step(n):
                        if n == steps[1]:
                            copy_outputs(it, 0, u)
                        if n == steps[3]:
                            squares(it, 1, u)
                            copy_x2(it, u)
                        if n == steps[4]:
                            copy_raw(it, 1, u)
                        if n == steps[5]:
                            guess_root(it, 1, u)
                        if n == steps[6]:
                            copy_queries(it, 1, u)
                    return at_step

                exponentials(it, 0, 1, second_layer(0, BESIDE_01))
                exponentials(it, 1, 0, second_layer(1, BESIDE_10))

                def finish_half(u, steps):
                    def at_step(n):
                        if n == steps[2]:
                            copy_outputs(it, 1, u)
                        if n == steps[4]:
                            square_z(it, u)
                        if n == steps[5]:
                            guess_norm(it, u)
                        if n == steps[6]:
                            copy_x1(it, u)
                        if n == steps[8]:
                            weight_ratio(it, u)
                    return at_step

                exponentials(it, 1, 1, finish_half(0, BESIDE_11))
                last_half = finish_half(1, AFTER)
                for n in range(len(AFTER)):
                    last_half(n)

            def silu(i, n):
                act.wait_ge(gate_ready, i + 1)
                nc.scalar.activation(sg[n], ps_s[:, n, 0:F], ACT.Silu).then_inc(silu_ready, 1)

            load_tables(act, SILU_SET)
            act.wait_ge(xs_turned, 1)
            nc.scalar.copy(xsT[0][:, :], ps_w[:, 0, 0:P]).then_inc(xsT_ready, 1)
            act.wait_ge(xs_turned, 2)
            nc.scalar.copy(xsT[1][:, :], ps_w[:, 0, 0:P]).then_inc(xsT_ready, 1)
            with act.Fori(0, (TILES - 1) // 2) as k:
                for n in range(2):
                    i = 2 * k + n
                    silu(i, n)
                    act.wait_ge(xs_turned, i + 3)
                    nc.scalar.copy(xsT[n][:, :], ps_w[:, 0, 0:P]).then_inc(xsT_ready, 1)
            silu(TILES - 1, 0)

            load_tables(act, LN_EXP_SET)
            for b in range(B):
                act.wait_ge(fin_c, b + 1)
                nc.scalar.activation(fin_z[b][0][:, :, :], fin_z[b][1][:, :, :], ACT.Square).then_inc(fin_sq, 1)
                act.wait_ge(fin_arg, b + 1)
                nc.scalar.activation(c_r[0][:, 4 * b:4 * b + 4], c_r[1][:, 4 * b:4 * b + 4], ACT.Ln).then_inc(act_own, 1)
                act.wait_ge(act_own, b + 1)
                nc.scalar.activation(c_r[0][:, 4 * b:4 * b + 4], c_r[0][:, 4 * b:4 * b + 4], ACT.Exp, scale=-0.5).then_inc(fin_guess, 1)

        @block.vector
        def _(dve):
            own = Chain(dve, dve_own)
            own.do(nc.vector.memset(pad_rows[:, :], 0.0))
            for u in range(HALVES):
                own.do(nc.vector.memset(x1[u][:, :, D:ROW], 0.0))
            own.do(nc.vector.memset(wacc[:, :, :], 0.0))
            dve.wait_ge(loaded["consts"], 16 * CONSTS)
            nc.vector.tensor_scalar(wqkv[:, 0, 0:D], wq1[:, :], norm_sb[:, 0:1], None, ALU.mult).then_inc(weights_ready, 1)
            nc.vector.tensor_scalar(wqkv[:, 1, :], wraw2[:, :], norm_sb[:, 1:2], None, ALU.mult).then_inc(weights_ready, 1)
            dve.wait_ge(fold_ready, 1)
            nc.vector.tensor_scalar(wqkv[:, 0, D:QKV], ps_w[:, 0, 0:QKV - D], norm_sb[:, 0:1], None, ALU.mult).then_inc(weights_ready, 1)
            own.do(nc.vector.tensor_copy(run[:, 0, :], expert_sb[:, 0:E]))
            own.sync()
            nc.vector.tensor_copy(pad_rows[:, D:D + 1], expert_sb[:, 2 * E:2 * E + 1]).then_inc(pad_set, 1)
            before_loop = own.n
            dve.wait_ge(pool_own, 14)

            def inverse_root(chain, y, v, a, b):
                chain.step(nc.vector.scalar_tensor_tensor(out=a, in0=y, scalar=-0.5, in1=v, op0=ALU.mult, op1=ALU.mult))
                chain.step(nc.vector.tensor_tensor(b, a, y, ALU.mult))
                return nc.vector.scalar_tensor_tensor(out=y, in0=b, scalar=1.5, in1=y, op0=ALU.add, op1=ALU.mult)

            def mean_squares(chain, it, l, u):
                dve.wait_ge(sq_ready[l][u].sem, sq_ready[l][u].at(it, 2))
                chain.do(nc.vector.tensor_reduce(ms[u][:, :, NH:NH + 1], xsq[u][:, :, :], AX.X, ALU.add))
                chain.step(nc.vector.tensor_reduce(ms[u][:, :, 0:NH], sq[u][:, :, :].rearrange("p t (h d) -> p t h d", d=HD), AX.X, ALU.add))
                x_ms = ms[u][:, :, NH:NH + 1]
                chain.step(nc.vector.tensor_scalar(x_ms, x_ms, 1.0 / D, RMS_EPS, ALU.mult, ALU.add))
                small = t_b[:, 0:QT].rearrange("p (t o) -> p t o", o=1)
                chain.step(nc.vector.tensor_scalar(small, x_ms, RMS_EPS, None, ALU.mult))
                tell(dve, nc.vector.scalar_tensor_tensor(out=ms[u][:, :, 0:NH], in0=ms[u][:, :, 0:NH], scalar=1.0 / HD,
                                                         in1=small.broadcast_to((P, QT, NH)), op0=ALU.mult, op1=ALU.add),
                     arg_ready[l][u], it, 1)

            def rotate(chain, it, l, u):
                dve.wait_ge(guess_ready[l][u].sem, guess_ready[l][u].at(it, 1))
                a3, b3 = (t[:, :].rearrange("p (t h) -> p t h", t=QT) for t in (t_a, t_b))
                tell(dve, inverse_root(chain, inv[u][:, :, :], ms[u][:, :, :], a3, b3), inv_ready[l][u], it, 1)
                root = inv[u][:, :, 0:NH].unsqueeze(3).broadcast_to((P, QT, NH, HD))
                chain.step(nc.vector.tensor_tensor(qn[:, :, :, :], raw[u][:, :, 0:NH * HD].rearrange("p t (h d) -> p t h d", d=HD), root, ALU.mult))
                val = raw[u][:, :, NH * HD:QKV].rearrange("p t (j d) -> p t j d", d=HD)
                row = inv[u][:, :, NH:NH + 1].unsqueeze(3).broadcast_to((P, QT, KVH, HD))
                if l == 0:
                    chain.do(nc.vector.tensor_tensor(v1[u][:, :, :, 0, 0:HD], val, row, ALU.mult))
                    nc.vector.tensor_tensor(v1[u][:, :, :, 1, 2 * HD:3 * HD], val, row, ALU.mult).then_inc(v_ready[0][u].sem, 1)
                else:
                    pairs = v2[u][:, :, :, :].rearrange("p (t o) j d -> p t o j d", o=2)
                    chain.step(nc.vector.tensor_tensor(pairs[:, :, 1, :, 0:HD], val, row, ALU.mult))
                    chain.do(nc.vector.tensor_copy(pairs[BLK:P, :, 0, :, 0:HD], pairs[0:BLK, :, 1, :, 0:HD]))
                    nc.vector.tensor_copy(pairs[0:BLK, 1:QT, 0, :, 0:HD], pairs[BLK:P, 0:QT - 1, 1, :, 0:HD]).then_inc(v_ready[1][u].sem, 1)
                half_heads = "p t h (o f) -> p t (h o) f"
                cos, sin = (rope_sb[:, l, n, :, :].unsqueeze(2).broadcast_to((P, QT, 2 * NH, HD // 2)) for n in range(2))
                q4 = qn[:, :, :, :].rearrange(half_heads, o=2)
                chain.do(nc.vector.tensor_tensor(by_cos[:, :, :, :].rearrange(half_heads, o=2), q4, cos, ALU.mult))
                chain.step(nc.vector.tensor_tensor(by_sin[:, :, :, :].rearrange(half_heads, o=2), q4, sin, ALU.mult))
                lo, hi = slice(0, HD // 2), slice(HD // 2, HD)
                chain.do(nc.vector.tensor_tensor(rot[:, :, :, lo], by_cos[:, :, :, lo], by_sin[:, :, :, hi], ALU.subtract))
                chain.step(nc.vector.tensor_tensor(rot[:, :, :, hi], by_sin[:, :, :, lo], by_cos[:, :, :, hi], ALU.add))
                x16 = qk16[u]
                chain.step(nc.vector.tensor_copy(x16[:, :, :, 0, :], rot[:, :, :, :]))
                chain.step(nc.vector.tensor_tensor(x16[:, :, :, 3, :], rot[:, :, :, :], x16[:, :, :, 0, :], ALU.subtract))
                for dst, src in ((1, 3), (2, 0)):
                    chain.do(nc.vector.tensor_copy(x16[:, :, 0:H, dst, :], x16[:, :, 0:H, src, :]))
                chain.do(nc.vector.tensor_copy(x16[:, :, H:NH, 1, :], x16[:, :, H:NH, 0, :]))
                tell(dve, nc.vector.tensor_copy(x16[:, :, H:NH, 2, :], x16[:, :, H:NH, 3, :]), split_ready[l][u], it, 1)

            def copy_heads(chain, it, l, u):
                dve.wait_ge(turned[l][u].sem, turned[l][u].at(it, 1))
                src = ps_w[:, 0, :].bitcast(F16).rearrange("p (c n) -> p c n", c=REP)
                nc.vector.tensor_copy(qT[u][:, :, 0:256], src).then_inc(qT_a[l][u].sem, 1)
                dve.wait_ge(turned[l][u].sem, turned[l][u].at(it, 3))
                for j in range(KVH):
                    rows_j = slice(HW * j, HW * j + HW)
                    last = nc.vector.tensor_copy(kT[u][rows_j, j, PAD:PAD + S], ps_w[rows_j, 0, :].bitcast(F16)[:, 0:S])
                    if j < KVH - 1:
                        chain.do(last)
                last.then_inc(kT_ready[l][u].sem, 1)

            def normalise(chain, it, l, u):
                if l == 0:
                    for cb in range(2):
                        dve.wait_ge(pv.sem, pv.at(it, first[0, u] + 12 * (cb + 1)))
                        tell(dve, nc.vector.tensor_copy(o_sb[0][cb][:, :], ps_o[:, cb, :]), o_out[0][u], it, cb + 1)
                    for n in range(2):
                        dve.wait_ge(o_turned[0][u].sem, o_turned[0][u].at(it, n + 1))
                        heads = ps_w[:, n, :].rearrange("p (a h) -> p a h", h=2 * HD)
                        den = rden[:, 0:4 * HD].rearrange("p (a o) -> p a o", o=1)
                        chain.step(nc.vector.reciprocal(den, heads[:, :, HD:HD + 1]))
                        dst = on[:, 2 * n:2 * n + 2, :].rearrange("p t (a d) -> p (t a) d", d=HD)
                        tell(dve, nc.vector.tensor_tensor(dst, heads[:, :, 0:HD], den.broadcast_to((P, 4 * HD, HD)), ALU.mult), on_part[0][u], it, n + 1)
                else:
                    for t in range(QT):
                        dve.wait_ge(o_turned[1][u].sem, o_turned[1][u].at(it, t + 1))
                        heads = ps_w[:, t % 2, :].rearrange("p (a h) -> p a h", h=HW)
                        den = rden[:, 0:H].rearrange("p (a o) -> p a o", o=1)
                        chain.step(nc.vector.reciprocal(den, heads[:, :, HD:HD + 1]))
                        dst = on[:, t, :].rearrange("p (a d) -> p a d", d=HD)
                        tell(dve, nc.vector.tensor_tensor(dst, heads[:, :, 0:HD], den.broadcast_to((P, H, HD)), ALU.mult), on_part[1][u], it, t + 1)

            def residual1(chain, it, u):
                dve.wait_ge(proj_ready[0][u].sem, proj_ready[0][u].at(it, 1))
                src = ps_w[:, 1, :].rearrange("p (t d) -> p t d", d=D)
                tell(dve, nc.vector.tensor_tensor(x2[u][:, :, :], src, x_in[u][:, :, :], ALU.add), x2_ready[u], it, 1)

            def residual2(chain, it, u):
                dve.wait_ge(proj_ready[1][u].sem, proj_ready[1][u].at(it, 1))
                src = ps_w[:, 1, :].rearrange("p (t d) -> p t d", d=D)
                tell(dve, nc.vector.tensor_tensor(z[:, :, :], src, x2[u][:, :, :], ALU.add), z_ready[u], it, 1)
                chain.step(nc.vector.tensor_tensor(z[:, :, :], z[:, :, :], x_in[u][:, :, :], ALU.add))
                total, mean, var, root = (ln_s[:, n, :].rearrange("p (t o) -> p t o", o=1) for n in range(4))
                chain.step(nc.vector.tensor_reduce(total, z[:, :, :], AX.X, ALU.add))
                chain.step(nc.vector.tensor_scalar(mean, total, 1.0 / D, None, ALU.mult))
                tell(dve, nc.vector.tensor_tensor(zc[:, :, :], z[:, :, :], mean.broadcast_to((P, QT, D)), ALU.subtract), zc_ready[u], it, 1)
                dve.wait_ge(zsq_ready[u].sem, zsq_ready[u].at(it, 1))
                chain.step(nc.vector.tensor_reduce(var, z[:, :, :], AX.X, ALU.add))
                tell(dve, nc.vector.tensor_scalar(var, var, 1.0 / D, LN_EPS, ALU.mult, ALU.add), zarg_ready[u], it, 1)
                dve.wait_ge(zguess_ready[u].sem, zguess_ready[u].at(it, 1))
                a3, b3 = (t[:, 0:QT].rearrange("p (t o) -> p t o", o=1) for t in (t_a, t_b))
                chain.step(inverse_root(chain, root, var, a3, b3))
                dve.wait_ge(x1_free[u].sem, x1_free[u].at(it, 0))
                ids_now = ids_sb[:, bass.ds((it * HALVES + u) * QT, QT)].rearrange("p (t o) -> p t o", o=1)
                chain.do(nc.vector.tensor_copy(x1[u][:, :, D:D + 1], ids_now))
                chain.sync()
                tell(dve, nc.vector.tensor_tensor(x1[u][:, :, 0:D], zc[:, :, :], root.broadcast_to((P, QT, D)), ALU.mult), x1_ready[u], it, 1)

            def choose(chain, it, u):
                dve.wait_ge(logits_ready[u].sem, logits_ready[u].at(it, 1))
                tell(dve, nc.vector.tensor_copy(lg[:, :, :], ps_w[:, 1, 0:QT * E].rearrange("p (t e) -> p t e", e=E)), logits_out[u], it, 1)
                order = expert_sb[:, E:2 * E].unsqueeze(1).broadcast_to((P, QT, E))
                s3 = [r_s[:, n, :].rearrange("p (t o) -> p t o", o=1) for n in range(8)]
                wide = [s.broadcast_to((P, QT, E)) for s in s3]
                src = lg
                for k in range(2):
                    chain.step(nc.vector.tensor_reduce(s3[k], src[:, :, :], AX.X, ALU.max))
                    chain.step(nc.vector.tensor_tensor(r_t[0][:, :, :], src[:, :, :], wide[k], ALU.is_ge))
                    chain.step(nc.vector.tensor_tensor(r_t[1][:, :, :], r_t[0][:, :, :], order, ALU.mult))
                    chain.step(nc.vector.tensor_reduce(s3[2 + k], r_t[1][:, :, :], AX.X, ALU.max))
                    chain.step(nc.vector.tensor_tensor(sel[k][:, :, :], r_t[1][:, :, :], wide[2 + k], ALU.is_equal))
                    if k == 0:
                        chain.step(nc.vector.scalar_tensor_tensor(out=r_t[2][:, :, :], in0=sel[0][:, :, :], scalar=-3e38,
                                                                  in1=lg[:, :, :], op0=ALU.mult, op1=ALU.add))
                        src = r_t[2]
                tell(dve, nc.vector.tensor_tensor(s3[4], s3[1], s3[0], ALU.subtract), gap_ready[u], it, 1)
                tell(dve, nc.vector.tensor_tensor(sel16[:, :, :], sel[0][:, :, :], sel[1][:, :, :], ALU.add), sel_ready[u], it, 1)
                dve.wait_ge(ratio_ready[u].sem, ratio_ready[u].at(it, 1))
                chain.step(nc.vector.tensor_scalar(s3[6], s3[5], 1.0, None, ALU.add))
                chain.step(nc.vector.reciprocal(s3[6], s3[6]))
                chain.step(nc.vector.tensor_tensor(s3[7], s3[5], s3[6], ALU.mult))
                for k in range(2):
                    chain.step(nc.vector.tensor_tensor(r_t[k][:, :, :], sel[k][:, :, :], wide[6 + k], ALU.mult))
                    chain.step(nc.vector.tensor_tensor(wacc[:, :, :], wacc[:, :, :], r_t[k][:, :, :], ALU.add))
                dve.wait_ge(ranks_ready[u].sem, ranks_ready[u].at(it, 1))
                for t in range(QT):
                    chain.step(nc.vector.tensor_tensor(run[:, t + 1, :], run[:, t, :], ps_w[:, 0, 64 + E * t:64 + E * t + E], ALU.add))
                tell(dve, nc.vector.tensor_tensor(r_t[3][:, :, :], run[:, 0:QT, :], ps_w[:, 0, 0:QT * E].rearrange("p (t e) -> p t e", e=E), ALU.add),
                     ranks_out[u], it, 1)
                chain.do(nc.vector.tensor_copy(run[:, 0, :], run[:, QT, :]))
                for k in range(2):
                    chain.step(nc.vector.tensor_tensor(r_t[k][:, :, :], sel[k][:, :, :], r_t[3][:, :, :], ALU.mult))
                    chain.step(nc.vector.tensor_reduce(s3[k], r_t[k][:, :, :], AX.X, ALU.add))
                both = r_s[:, 0:2, :]
                tell(dve, nc.vector.tensor_copy(slot[u][:, :, :], both), slots_ready[u], it, 1)

            for u in range(HALVES):
                for event in (arg_ready[0][u], v_ready[0][u], split_ready[0][u], x1_ready[u], logits_out[u], ranks_out[u]):
                    dve.sem_inc(event.sem, 1)
            with dve.Fori(0, PASSES) as it:
                chain = Chain(dve, dve_own, it, DVE_STEPS, before_loop)

                def prepare(l, u):
                    mean_squares(chain, it, l, u)
                    rotate(chain, it, l, u)
                    copy_heads(chain, it, l, u)

                prepare(0, 0)
                prepare(0, 1)
                normalise(chain, it, 0, 0)
                residual1(chain, it, 0)
                prepare(1, 0)
                normalise(chain, it, 0, 1)
                residual1(chain, it, 1)
                prepare(1, 1)
                normalise(chain, it, 1, 0)
                residual2(chain, it, 0)
                choose(chain, it, 0)
                normalise(chain, it, 1, 1)
                residual2(chain, it, 1)
                choose(chain, it, 1)
                assert chain.n == DVE_STEPS, chain.n

            own = Chain(dve, dve_own, 0, 0, before_loop + PASSES * DVE_STEPS)
            own.do(nc.vector.tensor_reduce(c_f[3][:, :], wacc[:, :, :].rearrange("p t e -> p e t"), AX.X, ALU.add))
            own.sync()
            nc.vector.tensor_copy(c_f[2][:, :], c_f[3][:, :]).then_inc(wsum_ready, 1)
            count, tiles, starts = c_f[0], c_f[1], c_f[2]
            base = expert_sb[:, 0:E]
            nc.vector.tensor_copy(end_sb[:, :], run[:, 0, :]).then_inc(tables, 1)
            own.step(nc.vector.tensor_tensor(count[:, :], run[:, 0, :], base, ALU.subtract))
            own.step(nc.vector.tensor_scalar(c_i[:, :], count[:, :], float(P - 1), None, ALU.add))
            own.step(nc.vector.tensor_scalar(c_i[:, :], c_i[:, :], 7, None, ALU.arith_shift_right))
            own.step(nc.vector.tensor_copy(tiles[:, :], c_i[:, :]))
            ends = c_t[0][:, 0, :]
            own.step(nc.vector.tensor_copy(ends[:, 0:1], tiles[:, 0:1]))
            for e in range(1, E):
                own.step(nc.vector.tensor_tensor(ends[:, e:e + 1], ends[:, e - 1:e], tiles[:, e:e + 1], ALU.add))
            dve.wait_ge(wsum_ready, 1)
            own.step(nc.vector.tensor_tensor(starts[:, :], ends, tiles[:, :], ALU.subtract))
            own.do(nc.vector.tensor_tensor(c_t[1][:, :, :], tile_no_sb[:, :, :], ends.unsqueeze(1).broadcast_to((P, TILES, E)), ALU.is_ge))
            own.step(nc.vector.tensor_tensor(c_t[2][:, :, :], tile_no_sb[:, :, :], starts[:, :].unsqueeze(1).broadcast_to((P, TILES, E)), ALU.is_ge))
            own.do(nc.vector.tensor_reduce(c_r[0][:, 0:TILES], c_t[1][:, :, :], AX.X, ALU.add))
            own.do(nc.vector.tensor_scalar(starts[:, :], starts[:, :], -float(P), None, ALU.mult))
            own.sync()
            own.do(nc.vector.tensor_tensor(starts[:, :], starts[:, :], base, ALU.add))
            own.step(nc.vector.tensor_tensor(c_t[2][:, :, :], c_t[2][:, :, :], c_t[1][:, :, :], ALU.subtract))
            own.step(nc.vector.scalar_tensor_tensor(out=c_t[0][:, :, :], in0=tile_no_sb[:, :, :], scalar=float(P),
                                                    in1=starts[:, :].unsqueeze(1).broadcast_to((P, TILES, E)), op0=ALU.mult, op1=ALU.add))
            own.step(nc.vector.tensor_tensor(c_t[0][:, :, :], c_t[0][:, :, :], c_t[2][:, :, :], ALU.mult))
            own.do(nc.vector.tensor_reduce(c_r[1][:, 0:TILES], c_t[0][:, :, :], AX.X, ALU.add))
            own.step(nc.vector.memset(c_r[1][:, TILES:TILES + 1], float(PADROW)))
            past = c_t[1][:, :, E - 1]
            own.step(nc.vector.scalar_tensor_tensor(out=c_r[1][:, 0:TILES], in0=past, scalar=float(PADROW), in1=c_r[1][:, 0:TILES], op0=ALU.mult, op1=ALU.add))
            nc.vector.tensor_copy(row_sb[:, :], c_r[1][:, :]).then_inc(tables, 1)
            own.step(nc.vector.memset(c_r[0][:, TILES:TILES + 1], 0.0))
            own.step(nc.vector.tensor_scalar(c_r[0][:, :], c_r[0][:, :], float(E - 1), None, ALU.min))
            nc.vector.tensor_copy(te_sb[:, :], c_r[0][:, :]).then_inc(tables, 1)
            own.step(nc.vector.tensor_scalar(count[:, :], count[:, :], 1.0, None, ALU.max))
            own.step(nc.vector.reciprocal(count[:, :], count[:, :]))
            dve.wait_ge(counted, 1)
            own.step(nc.vector.tensor_tensor(mean_w[:, :], ps_w[:, 1, 0:E], count[:, :], ALU.mult))
            dve.wait_ge(tables, 3)

            def hidden(i, n):
                dve.wait_ge(silu_ready, i + 1)
                dve.wait_ge(up_ready, i + 1)
                nc.vector.tensor_tensor(hid[n], sg[n], ps_s[:, n, F:2 * F], ALU.mult).then_inc(hid_ready, 1)

            def copy_hidden(i, n):
                dve.wait_ge(hid_turned, i + 1)
                nc.vector.tensor_copy(hT[n], ps_o[:, n, :]).then_inc(hT_ready, 1)

            def keep_ids(i, n, pair):
                dve.wait_ge(xs_loaded[n], 16 * (pair + 1))
                nc.vector.tensor_copy(tile_ids[:, bass.ds(i, 1)], xs[n][:, D:D + 1]).then_inc(ids_kept, 1)

            def weigh(i, n):
                e = dve.value_load(te_sb[0:1, bass.ds(i, 1)], min_val=0, max_val=E - 1)
                dve.wait_ge(y_ready, i + 1)
                dve.wait_ge(ids_kept, i + 1)
                nc.vector.tensor_copy(idu[n][:, :], tile_ids[:, bass.ds(i, 1)]).then_inc(idu_ready, 1)
                nc.vector.tensor_scalar(ys[n][:, :], ps_w[:, 1, 0:D], mean_w[:, bass.ds(e, 1)], None, ALU.mult).then_inc(ys_ready, 1)

            keep_ids(0, 0, 0)
            keep_ids(1, 1, 0)
            hidden(0, 0)

            def tile_pair(k, first=False):
                for n in range(2):
                    i = 2 * k + n
                    copy_hidden(i, n)
                    hidden(i + 1, 1 - n)
                    keep_ids(i + 2, n, k + 1)
                    if not first:
                        dve.wait_ge(added, 16 * (i - 1))
                    weigh(i, n)

            tile_pair(0, first=True)
            with dve.Fori(1, (TILES - 1) // 2) as k:
                tile_pair(k)
            copy_hidden(TILES - 1, 0)
            dve.wait_ge(added, 16 * (TILES - 2))
            weigh(TILES - 1, 0)

            own = Chain(dve, dve_own, 0, 0, before_loop + PASSES * DVE_STEPS + own.n)
            for b in range(B):
                src, cen = fin_z[b]
                dve.wait_ge(fin_loaded[b], 16)
                total, mean = (t[:, 8 * n:8 * n + QT].rearrange("p (t o) -> p t o", o=1) for n, t in enumerate((t_a, t_a)))
                var, root = (c_r[n][:, 4 * b:4 * b + 4].rearrange("p (t o) -> p t o", o=1) for n in (1, 0))
                own.step(nc.vector.tensor_reduce(total, src[:, :, :], AX.X, ALU.add))
                own.step(nc.vector.tensor_scalar(mean, total, 1.0 / D, None, ALU.mult))
                nc.vector.tensor_tensor(cen[:, :, :], src[:, :, :], mean.broadcast_to((P, QT, D)), ALU.subtract).then_inc(fin_c, 1)
                dve.wait_ge(fin_sq, b + 1)
                own.step(nc.vector.tensor_reduce(var, src[:, :, :], AX.X, ALU.add))
                nc.vector.tensor_scalar(var, var, 1.0 / D, LN_EPS, ALU.mult, ALU.add).then_inc(fin_arg, 1)
                dve.wait_ge(fin_guess, b + 1)
                a3, b3 = (t[:, 16:16 + QT].rearrange("p (t o) -> p t o", o=1) for t in (t_a, t_b))
                own.step(inverse_root(own, root, var, a3, b3))
                nc.vector.tensor_tensor(src[:, :, :], cen[:, :, :], root.broadcast_to((P, QT, D)), ALU.mult).then_inc(fin_ready, 1)


SILU_SET = 18
LN_EXP_SET = 6
ATTN_LOADS = 5
BESIDE_01 = (1, 4, 6, 8, 9, 13, 21, 22)
BESIDE_10 = (0, 2, 3, 4, 5, 6, 10, 10)
BESIDE_11 = (0, 1, 2, 3, 4, 5, 6, 7, 10)
AFTER = (0, 1, 2, 3, 4, 5, 6, 7, 8)
CONSTS = 10
DVE_STEPS = 164


def kernel(**inputs):
    import concourse.bacc as bacc
    from concourse.bass_utils import run_bass_kernel_spmd

    a = {name.removeprefix("L0_attn_").removeprefix("L0_ffn_"): np.asarray(v) for name, v in inputs.items()}
    tokens = a["hidden"].reshape(T, D)
    head_of = np.array([[KVH * j + c for j in range(KVH)] for c in range(REP)]).reshape(-1)
    pair_first = np.concatenate([np.arange(0, HD, 2), np.arange(1, HD, 2)])
    q_cols = (head_of[:, None] * HD + pair_first[None, :]).reshape(-1)
    k_cols = (np.arange(KVH)[:, None] * HD + pair_first[None, :]).reshape(-1)
    wide_heads = np.array([[[KVH * j + 2 * cb + pl for pl in range(2)] for j in range(KVH)] for cb in range(2)]).reshape(-1)
    g_rows, l_rows = ((h[:, None] * HD + np.arange(HD)[None, :]).reshape(-1) for h in (wide_heads, head_of))
    con = constants()
    ins = {
        "x_tok": tokens,
        "x_feat": tokens.T,
        "w_qkv1": a["g_wq"][:, q_cols],
        "w_kv_down_t": a["g_kv_down"].T,
        "w_kv_up": np.concatenate([a["g_k_up"][:, k_cols], a["g_v_up"]], 1),
        "w_qkv2": np.concatenate([a["l_wq"][:, q_cols], a["l_wk"][:, k_cols], a["l_wv"]], 1),
        "wo": np.concatenate([a["g_wo"][g_rows], a["l_wo"][l_rows]], 1),
        "norm_w": np.stack([a["norm1_w"], a["norm2_w"]], 1),
        "router_t": a["router_w"].T,
        "gate_t": a["gate_w"].transpose(2, 0, 1).reshape(D, E * F),
        "up_t": a["up_w"].transpose(2, 0, 1).reshape(D, E * F),
        "down_t": a["down_w"].transpose(2, 0, 1).reshape(FC, P, E, D).transpose(1, 2, 0, 3).reshape(P, E * FC * D),
        **con,
    }
    nc = bacc.Bacc("TRN2", target_bir_lowering=False, num_devices=1)
    arrays, args = {}, {}
    for name, v in ins.items():
        arrays[f"in_{name}"] = np.ascontiguousarray(v)
        args[name] = nc.dram_tensor(f"in_{name}", v.shape, mybir.dt.from_np(v.dtype), kind="ExternalInput").ap()
    args["out"] = nc.dram_tensor("out_0", (B, S, D), F32, kind="ExternalOutput").ap()
    block_program(nc, **args)
    return run_bass_kernel_spmd(nc, [arrays], core_ids=[0]).results[0]["out_0"]
```
